# Optimizing a Trainium2 kernel written in Bass

```python
import numpy as np
import jax
import jax.numpy as jnp

def _softmax(x, axis=-1):
    return jax.nn.softmax(x, axis=axis)

def _gelu(x):
    return jax.nn.gelu(x, approximate=True)

def _silu(x):
    return jax.nn.silu(x)

def _sigmoid(x):
    return jax.nn.sigmoid(x)

def _layernorm(x, axis=-1, eps=1e-05):
    m = jnp.mean(x, axis=axis, keepdims=True)
    v = jnp.var(x, axis=axis, keepdims=True)
    return (x - m) / jnp.sqrt(v + eps)

def _scatter_add(tgt, idx, src, axis=0):
    return tgt.at[idx].add(src)

def _segment_sum(src, seg, n):
    return jax.ops.segment_sum(src, seg, n)
kernel_name = 'mk_vit_tower_postln_d1_tok_img256_r4_887709'

def setup_inputs(seed: int=0):
    np.random.seed(seed)
    _w = jnp.asarray

    def _rec_inputs():
        import jax
        import jax.numpy as jnp
        _rk = jax.random.key(seed)
        x = -7.10856e-05 + 0.999911 * jax.random.normal(jax.random.fold_in(_rk, 1), (4, 64, 128, 64), jnp.float32)
        return x
    x = _rec_inputs()

    def _L0_tok_setup():
        import jax, jax.numpy as jnp
        import numpy as np
        PATCH_LEN = 16
        STRIDE = 8
        PAD = 8
        key = jax.random.key(seed)
        k1, k2 = jax.random.split(key)
        x = jax.random.normal(k1, (32, 64, 128, 64), dtype=jnp.float32)
        in_feat = 64 * (PATCH_LEN // 2 + 1) * 2
        W = jax.random.normal(k2, (64, in_feat), dtype=jnp.float32) * 0.02
        return {'x': x, 'W': W}
    _L0_tok_all = _L0_tok_setup()
    _L0_tok_in = {k: v for k, v in _L0_tok_all.items() if k in ('W',)}
    del _L0_tok_all

    def _L0_attn_setup():
        import jax, jax.numpy as jnp
        import numpy as np
        NEG_INF = 1e+32
        key = jax.random.key(seed)
        ks = jax.random.split(key, 7)
        B, S, C, DK, DO = (16, 512, 64, 64, 64)
        sc = 1.0 / np.sqrt(C)
        return {'x': jax.random.normal(ks[0], (B, S, C), jnp.float32), 'Wq': jax.random.normal(ks[1], (C, DK), jnp.float32) * sc, 'bq': jnp.zeros((DK,), jnp.float32), 'Wk': jax.random.normal(ks[2], (C, DK), jnp.float32) * sc, 'bk': jnp.zeros((DK,), jnp.float32), 'Wv': jax.random.normal(ks[3], (C, DO), jnp.float32) * sc, 'bv': jnp.zeros((DO,), jnp.float32)}
    _L0_attn_all = _L0_attn_setup()
    _L0_attn_in = {k: v for k, v in _L0_attn_all.items() if k in ('Wq', 'bq', 'Wk', 'bk', 'Wv', 'bv')}
    del _L0_attn_all

    def _L0_ffn_setup():
        import jax, jax.numpy as jnp
        import numpy as np
        DIM = 64
        HEADS = 8
        NUM_KEYS = 64
        NUM_KV = NUM_KEYS ** 2
        PK_TOPK = 16
        FINAL_TOPK = 16
        DIM_KEY = DIM // 2
        P = 2

        def _pk(x, Wq_pk, pk_keys):
            b, n, _ = x.shape
            q = (x @ Wq_pk).reshape(b, n, P, HEADS, DIM_KEY).transpose(2, 0, 1, 3, 4)
            sim = jnp.einsum('pbnhd,pkhd->pbnhk', q, pk_keys)
            scores, idx = jax.lax.top_k(sim, PK_TOPK)
            idx0 = idx[0]
            idx1 = idx[1] * NUM_KEYS
            index = (idx0[..., :, None] + idx1[..., None, :]).reshape(b, n, HEADS, PK_TOPK * PK_TOPK)
            score = (scores[0][..., :, None] + scores[1][..., None, :]).reshape(b, n, HEADS, PK_TOPK * PK_TOPK)
            final_scores, pk_idx = jax.lax.top_k(score, FINAL_TOPK)
            final_indices = jnp.take_along_axis(index, pk_idx, axis=-1)
            final_scores = jax.nn.softmax(final_scores, axis=-1)
            return (final_scores, final_indices)
        key = jax.random.key(seed)
        ks = jax.random.split(key, 7)
        b, n = (2, 256)
        std = 0.02
        x = jax.random.normal(ks[0], (b, n, DIM), dtype=jnp.float32)
        Wq_pk = jax.random.normal(ks[1], (DIM, P * HEADS * DIM_KEY), dtype=jnp.float32) * std
        pk_keys = jax.random.normal(ks[2], (P, NUM_KEYS, HEADS, DIM_KEY), dtype=jnp.float32) * std
        Wq = jax.random.normal(ks[3], (DIM, HEADS * DIM), dtype=jnp.float32) * std
        keys_table = jax.random.normal(ks[4], (NUM_KV * HEADS, DIM), dtype=jnp.float32) * std
        values_table = jax.random.normal(ks[5], (NUM_KV * HEADS, DIM), dtype=jnp.float32) * std
        Wo = jax.random.normal(ks[6], (DIM * HEADS, DIM), dtype=jnp.float32) * std
        return {'x': x, 'Wq_pk': Wq_pk, 'pk_keys': pk_keys, 'Wq': Wq, 'keys_table': keys_table, 'values_table': values_table, 'Wo': Wo}
    _L0_ffn_all = _L0_ffn_setup()
    _L0_ffn_in = {k: v for k, v in _L0_ffn_all.items() if k in ('Wq_pk', 'pk_keys', 'Wq', 'keys_table', 'values_table', 'Wo')}
    del _L0_ffn_all
    return {'x': x, 'L0_tok_W': _L0_tok_in['W'], 'L0_attn_Wq': _L0_attn_in['Wq'], 'L0_attn_bq': _L0_attn_in['bq'], 'L0_attn_Wk': _L0_attn_in['Wk'], 'L0_attn_bk': _L0_attn_in['bk'], 'L0_attn_Wv': _L0_attn_in['Wv'], 'L0_attn_bv': _L0_attn_in['bv'], 'L0_ffn_Wq_pk': _L0_ffn_in['Wq_pk'], 'L0_ffn_pk_keys': _L0_ffn_in['pk_keys'], 'L0_ffn_Wq': _L0_ffn_in['Wq'], 'L0_ffn_keys_table': _L0_ffn_in['keys_table'], 'L0_ffn_values_table': _L0_ffn_in['values_table'], 'L0_ffn_Wo': _L0_ffn_in['Wo']}

def reference(x, L0_tok_W, L0_attn_Wq, L0_attn_bq, L0_attn_Wk, L0_attn_bk, L0_attn_Wv, L0_attn_bv, L0_ffn_Wq_pk, L0_ffn_pk_keys, L0_ffn_Wq, L0_ffn_keys_table, L0_ffn_values_table, L0_ffn_Wo):
    import jax
    import jax.numpy as jnp

    def _L0_tok_ref(x, W):
        import jax, jax.numpy as jnp
        import numpy as np
        PATCH_LEN = 16
        STRIDE = 8
        PAD = 8
        B, C, T, V = x.shape
        xp = jnp.pad(x, ((0, 0), (0, 0), (0, PAD), (0, 0)), mode='edge')
        Tp = T + PAD
        N = (Tp - PATCH_LEN) // STRIDE + 1
        idx = jnp.arange(N)[:, None] * STRIDE + jnp.arange(PATCH_LEN)[None, :]
        patches = xp[:, :, idx, :]
        patches = jnp.transpose(patches, (0, 4, 2, 3, 1))
        xf = jnp.fft.rfft(patches, axis=-2, norm='ortho')
        F = xf.shape[-2]
        x_real = xf.real.reshape(B, V, N, F * C)
        x_imag = xf.imag.reshape(B, V, N, F * C)
        x_emb = jnp.concatenate([x_real, x_imag], axis=-1)
        x_emb = x_emb @ W.T
        return x_emb.reshape(B, V * N, -1)

    def _L0_attn_ref(x, Wq, bq, Wk, bk, Wv, bv):
        import jax, jax.numpy as jnp
        import numpy as np
        NEG_INF = 1e+32
        dk = Wq.shape[-1]
        Q = x @ Wq + bq
        K = x @ Wk + bk
        V = x @ Wv + bv
        attn = jnp.einsum('bqd,bkd->bqk', Q, K) / jnp.sqrt(jnp.float32(dk))
        S = attn.shape[1]
        causal = jnp.tril(jnp.ones((S, S), jnp.float32))
        attn = causal * attn + (1.0 - causal) * -NEG_INF
        probs = jax.nn.softmax(attn, axis=2)
        return jnp.einsum('bqk,bkd->bqd', probs, V)

    def _L0_ffn_ref(x, Wq_pk, pk_keys, Wq, keys_table, values_table, Wo):
        import jax, jax.numpy as jnp
        import numpy as np
        DIM = 64
        HEADS = 8
        NUM_KEYS = 64
        NUM_KV = NUM_KEYS ** 2
        PK_TOPK = 16
        FINAL_TOPK = 16
        DIM_KEY = DIM // 2
        P = 2

        def _pk(x, Wq_pk, pk_keys):
            b, n, _ = x.shape
            q = (x @ Wq_pk).reshape(b, n, P, HEADS, DIM_KEY).transpose(2, 0, 1, 3, 4)
            sim = jnp.einsum('pbnhd,pkhd->pbnhk', q, pk_keys)
            scores, idx = jax.lax.top_k(sim, PK_TOPK)
            idx0 = idx[0]
            idx1 = idx[1] * NUM_KEYS
            index = (idx0[..., :, None] + idx1[..., None, :]).reshape(b, n, HEADS, PK_TOPK * PK_TOPK)
            score = (scores[0][..., :, None] + scores[1][..., None, :]).reshape(b, n, HEADS, PK_TOPK * PK_TOPK)
            final_scores, pk_idx = jax.lax.top_k(score, FINAL_TOPK)
            final_indices = jnp.take_along_axis(index, pk_idx, axis=-1)
            final_scores = jax.nn.softmax(final_scores, axis=-1)
            return (final_scores, final_indices)
        b, n, d = x.shape
        q = (x @ Wq).reshape(b, n, HEADS, DIM) * DIM ** (-0.5)
        kv_scores, indices = _pk(x, Wq_pk, pk_keys)
        offsets = jnp.arange(HEADS, dtype=indices.dtype) * NUM_KV
        ind = indices + offsets[None, None, :, None]
        k = jnp.einsum('bnhk,bnhkd->bnhd', kv_scores, keys_table[ind])
        v = jnp.einsum('bnhk,bnhkd->bnhd', kv_scores, values_table[ind])
        sim = jnp.einsum('bihd,bjhd->bhij', q, k)
        neg = -jnp.finfo(sim.dtype).max
        causal = jnp.tril(jnp.ones((n, n), dtype=bool))
        sim = jnp.where(causal, sim, neg)
        attn = jax.nn.softmax(sim, axis=-1)
        out = jnp.einsum('bhij,bjhd->bhid', attn, v)
        out = out.transpose(0, 2, 1, 3).reshape(b, n, HEADS * DIM)
        return out @ Wo
    h = _L0_tok_ref(x, L0_tok_W)
    h = _layernorm(h + _L0_attn_ref(h, L0_attn_Wq, L0_attn_bq, L0_attn_Wk, L0_attn_bk, L0_attn_Wv, L0_attn_bv), axis=-1)
    h = _layernorm(h + _L0_ffn_ref(h, L0_ffn_Wq_pk, L0_ffn_pk_keys, L0_ffn_Wq, L0_ffn_keys_table, L0_ffn_values_table, L0_ffn_Wo), axis=-1)
    return h

_drawn_inputs = setup_inputs


def setup_inputs(seed=0):
    import zlib

    import numpy as np

    out = dict(_drawn_inputs(seed))
    spreads = {'L0_attn_bq': (0.0, 0.8), 'L0_attn_bk': (0.0, 2.0), 'L0_attn_bv': (0.0, 0.1)}
    factors = {'L0_ffn_Wq_pk': 25.234,
     'L0_ffn_pk_keys': 24.19,
     'L0_ffn_Wq': 64.0,
     'L0_ffn_keys_table': 64.0,
     'L0_ffn_values_table': 22.009,
     'L0_ffn_Wo': 21.385}
    for name, (base, spread) in spreads.items():
        noise = np.random.default_rng([zlib.crc32(name.encode()), seed]).standard_normal(out[name].shape)
        drawn = base * np.exp(spread * noise) if base else spread * noise
        out[name] = jnp.asarray(drawn.astype(out[name].dtype))
    for name, factor in factors.items():
        out[name] = (out[name] * factor).astype(out[name].dtype)
    return out
```

```python
from contextlib import ExitStack

import concourse.bass as bass
from concourse import mybir

F32, BF16, U32 = mybir.dt.float32, mybir.dt.bfloat16, mybir.dt.uint32
ALU = mybir.AluOpType
ACT = mybir.ActivationFunctionType
AX_X = mybir.AxisListType.X

B, C, T, V = 4, 64, 128, 64
PATCH, STRIDE = 16, 8
N = T // STRIDE
S = V * N
P = 128
TPB = S // P
TILES = B * TPB
VT = P // N
D = 64
FREQS = PATCH // 2 + 1
H, NK, TOPK, DK = 8, 64, 16, 32
NKV = NK * NK
KV = 2 * D
SCALE = D ** -0.5
EPS = 1e-5
NEWTON = 3
NORM_STEPS = 4 + 3 * NEWTON
NEG = -1e30
LOW = -3e38
SLOTS = 4
GROUP = 4

BLOCKS = [(0, 1, 16), (1, 1, 8), (2, 2, 5), (4, 4, 3), (8, 8, 1)]
CAND = sum(nr * nc_ for _, nr, nc_ in BLOCKS)


def build(nc, x, w_tok, w_qkv, w_pk, keys, w_q, table, w_o, dft, ident_d, mask_d, iota_d, hbase_d, out):
    with ExitStack() as ctx:
        def sb(name, shape, dt=F32):
            return ctx.enter_context(nc.sbuf_tensor(name, shape, dt))

        def ps(name, shape):
            return ctx.enter_context(nc.psum_tensor(name, shape, F32))

        def sem(name):
            return ctx.enter_context(nc.semaphore(name))

        ident = sb("ident", [P, P])
        mask = sb("mask", [P, S - P + S])
        iota = sb("iota", [P, CAND, TOPK], BF16)
        hbase = sb("hbase", [P, H, TOPK])
        dftm = sb("dftm", [4 * FREQS, STRIDE])
        weff = sb("weff", [P, STRIDE, D])
        wqkv = sb("wqkv", [D + 1, 3, D])
        wpk = sb("wpk", [DK, 2 * H, D])
        keysT = sb("keysT", [DK, 2 * H, NK])
        msim = sb("msim", [D, 2 * H * NK])
        wffq = sb("wffq", [D, H * D])
        wo = sb("wo", [P, 4, D])
        k1T = sb("k1T", [D, S])
        v1 = sb("v1", [P, TPB, D])
        kT = sb("kT", [D, H, S])
        vs = sb("vs", [P, TPB, H, D])
        xin = sb("xin", [P, T * VT])
        hT = sb("hT", [D + 1, P])
        hn = sb("hn", [P, D])
        q1T = sb("q1T", [D, P])
        mask1 = sb("mask1", [P, S])
        mask2 = sb("mask2", [P, S])
        sm = sb("sm", [P, S])
        prob = sb("prob", [P, S])
        pT = sb("pT", [P, S])
        col = sb("col", [P, 16])
        y1 = sb("y1", [P, D])
        x1 = sb("x1", [P, D])
        x1c = sb("x1c", [P, D])
        x1T = sb("x1T", [D, P])
        sims = sb("sims", [P, 2, H, NK])
        rest = sb("rest", [P, 2, GROUP, NK])
        rs = sb("rs", [P, 2, GROUP, TOPK])
        ri = sb("ri", [P, 2, GROUP, TOPK], U32)
        code1 = sb("code1", [P, GROUP, TOPK])
        cs = sb("cs", [P, GROUP, CAND])
        cs2 = sb("cs2", [P, GROUP, CAND])
        cc = sb("cc", [P, GROUP, CAND])
        fs = sb("fs", [P, GROUP, TOPK])
        fd = sb("fd", [P, GROUP, TOPK])
        fe = sb("fe", [P, GROUP, TOPK])
        pos = sb("pos", [P, GROUP, TOPK], U32)
        posb = sb("posb", [P, GROUP, TOPK], BF16)
        eq = sb("eq", [P, GROUP, CAND, TOPK], BF16)
        pick = sb("pick", [P, GROUP, CAND, TOPK])
        fsum = sb("fsum", [P, 2, GROUP])
        idx = sb("idx", [P, H, TOPK], U32)
        wgt = sb("wgt", [P, H, TOPK])
        G = sb("G", [P, SLOTS, TOPK, KV])
        wtok = G[0:4 * FREQS].rearrange("p s k (h c) -> p (s k) (h c)", c=C)
        kn = sb("kn", [P, D])
        qT = sb("qT", [D, H, P])
        on = sb("on", [P, H * D])
        oT = sb("oT", [P, 4, P])
        col2 = sb("col2", [P, 16])
        y2 = sb("y2", [P, D])
        yo = sb("yo", [P, D])

        psS = ps("psS", [P, S])
        psT = ps("psT", [P, S])
        psA = ps("psA", [P, 512])
        psK = ps("psK", [P, 512])
        psO = ps("psO", [P, H * D])
        psF = ps("psF", [P, 512])

        c_loaded = sem("c_loaded")
        zeroed = sem("zeroed")
        wtok_zeroed = sem("wtok_zeroed")
        prep_pe = sem("prep_pe")
        prep_act = sem("prep_act")
        x_loaded = sem("x_loaded")
        tok_done = sem("tok_done")
        hT_ready = sem("hT_ready")
        proj_done = sem("proj_done")
        qkv_ready = sem("qkv_ready")
        mask1_ready = sem("mask1_ready")
        mask2_ready = sem("mask2_ready")
        s1_done = sem("s1_done")
        s1_masked = sem("s1_masked")
        p1_ready = sem("p1_ready")
        p1T_done = sem("p1T_done")
        p1T_ready = sem("p1T_ready")
        pv1_done = sem("pv1_done")
        x1_ready = sem("x1_ready")
        x1T_done = sem("x1T_done")
        x1T_ready = sem("x1T_ready")
        sims_done = sem("sims_done")
        sims_ready = sem("sims_ready")
        fd_ready = sem("fd_ready")
        fe_ready = sem("fe_ready")
        routed = sem("routed")
        gathered = [sem(f"gathered{i}") for i in range(SLOTS)]
        weighted = sem("weighted")
        combined = sem("combined")
        kv_copied = sem("kv_copied")
        kT_done = sem("kT_done")
        kT_ready = sem("kT_ready")
        qT_done = sem("qT_done")
        qT_ready = sem("qT_ready")
        s2_done = sem("s2_done")
        s2_masked = sem("s2_masked")
        p2_ready = sem("p2_ready")
        p2T_done = sem("p2T_done")
        p2T_ready = sem("p2T_ready")
        pv2_done = sem("pv2_done")
        o_ready = sem("o_ready")
        oT_done = sem("oT_done")
        oT_ready = sem("oT_ready")
        wo_done = sem("wo_done")
        y_ready = sem("y_ready")
        stored = sem("stored")
        front_step = sem("front_step")
        route_step = sem("route_step")
        mix_step = sem("mix_step")
        own_waits = sem("own_waits")
        back_step = sem("back_step")

        consts = [
            (ident[:], ident_d), (mask[:], mask_d), (iota[:].rearrange("p c k -> p (c k)"), iota_d),
            (hbase[:].rearrange("p h k -> p (h k)"), hbase_d), (dftm[:], dft),
            (wqkv[:], w_qkv), (wpk[:], w_pk), (keysT[:], keys), (wffq[:], w_q),
            (wo[:], w_o.rearrange("(c p) o -> p c o", p=P)),
        ]
        w_rows = w_tok.rearrange("o (r c) -> r o c", c=C)
        n_rows = 2 * FREQS

        block = ctx.enter_context(nc.Block())

        def tile_in_batch(t):
            return t % TPB

        def own(engine):
            engine.sem_inc(own_waits, 1)

        @block.sync
        def _(sp):
            def load_x(t):
                src = x[bass.ds(t, 1)].rearrange("o c s v -> (o c) s v")
                view = xin[:].rearrange("p (s v) -> p s v", v=VT)
                sp.dma_start(view[0:C], src).then_inc(x_loaded, 16)
                sp.dma_start(view[C:P, 0:T - STRIDE], src[:, STRIDE:T]).then_inc(x_loaded, 16)
                sp.dma_start(view[C:P, T - STRIDE:T],
                             src[:, T - 1:T].broadcast_to([C, STRIDE, VT])).then_inc(x_loaded, 16)

            load_x(0)
            sp.wait_ge(wtok_zeroed, 1)
            sp.dma_start(wtok[0:n_rows, :, 0:C], w_rows).then_inc(c_loaded, 16)
            sp.dma_start(wtok[n_rows:2 * n_rows, :, C:P], w_rows).then_inc(c_loaded, 16)
            for dst, src in consts:
                sp.dma_start(dst, src).then_inc(c_loaded, 16)
            sp.wait_ge(tok_done, 1)
            load_x(1)

            def store(t):
                sp.wait_ge(y_ready, t + 1)
                own(sp)
                sp.dma_start(out[bass.ds(t, 1)].rearrange("o p d -> (o p) d"), yo[:]).then_inc(stored, 16)
                sp.wait_ge(stored, 16 * t + 16)
                own(sp)

            with sp.Fori(0, TILES - 2) as t:
                store(t)
                sp.wait_ge(tok_done, t + 2)
                own(sp)
                load_x(t + 2)
            store(TILES - 2)
            store(TILES - 1)

        @block.gpsimd
        def _(pool):
            nc.gpsimd.memset(vs[:], 0.0)
            nc.gpsimd.memset(kT[:], 0.0).then_inc(zeroed, 1)

            def gathers(t, first):
                for h in range(H):
                    if h % GROUP == 0:
                        pool.wait_ge(routed, 2 * t + h // GROUP + 1)
                    if not (first and h < SLOTS):
                        pool.wait_ge(combined, H * t + h - SLOTS + 1)
                    own(pool)
                    for k in range(TOPK):
                        pool.indirect_dma_start(
                            G[:, h % SLOTS, k, :], None, table,
                            bass.IndirectOffsetOnAxis(idx[:, h, k:k + 1], 0),
                        ).then_inc(gathered[h % SLOTS], 16)

            gathers(0, True)
            with pool.Fori(1, TILES) as t:
                gathers(t, False)

        @block.tensor
        def _(pe):
            def scores_T(done):
                for j in range(TPB):
                    last = pe.transpose(psT[:, j * P:(j + 1) * P], prob[:, j * P:(j + 1) * P], ident[:])
                last.then_inc(done, 1)

            pe.wait_ge(c_loaded, 16 * (2 + len(consts)))
            for o in range(D):
                pe.matmul(psS[:, o * STRIDE:(o + 1) * STRIDE], wtok[:, o, :], dftm[:], start=True, stop=True)
            for i in range(2 * H):
                last = pe.matmul(psT[0:D, i * NK:(i + 1) * NK], wpk[:, i, :], keysT[:, i, :], start=True, stop=True)
            last.then_inc(prep_pe, 1)
            pe.wait_ge(prep_act, 1)

            def front(t):
                pe.wait_ge(x_loaded, 48 * t + 48)
                xv = xin[:].rearrange("p (n s v) -> p s v n", s=STRIDE, v=VT)
                for s in range(STRIDE):
                    last = pe.matmul(psA[0:D, 0:P], weff[:, s, :], xv[:, s], start=(s == 0), stop=(s == STRIDE - 1))
                last.then_inc(tok_done, 1)
                pe.wait_ge(hT_ready, t + 1)
                pe.matmul(psA[0:D, 128:256], wqkv[:, 0, :], hT[:], start=True, stop=True)
                pe.matmul(psA[0:D, 256:384], wqkv[:, 1, :], hT[:], start=True, stop=True)
                pe.matmul(psA[:, 384:448], hT[:], wqkv[:, 2, :], start=True, stop=True)
                pe.transpose(psA[:, 448:512], hT[0:D, :], ident[0:D, 0:D]).then_inc(proj_done, 1)
                pe.wait_ge(qkv_ready, t + 1)
                for j in range(2):
                    last = pe.matmul(psS[:, j * 512:(j + 1) * 512], q1T[:], k1T[:, j * 512:(j + 1) * 512],
                                     start=True, stop=True)
                last.then_inc(s1_done, 1)
                pe.wait_ge(p1_ready, t + 1)
                scores_T(p1T_done)
                pe.wait_ge(p1T_ready, t + 1)
                for j in range(TPB):
                    last = pe.matmul(psF[:, 0:D], pT[:, j * P:(j + 1) * P], v1[:, j, :],
                                     start=(j == 0), stop=(j == TPB - 1))
                last.then_inc(pv1_done, 1)
                pe.wait_ge(x1_ready, t + 1)
                own(pe)
                pe.transpose(psK[0:D, 256:384], x1[:], ident[:]).then_inc(x1T_done, 1)
                pe.wait_ge(x1T_ready, t + 1)
                for j in range(2):
                    last = pe.matmul(psS[:, j * 512:(j + 1) * 512], x1T[:], msim[:, j * 512:(j + 1) * 512],
                                     start=True, stop=True)
                last.then_inc(sims_done, 1)

            def queries(t):
                for h in range(H):
                    last = pe.matmul(psT[0:D, h * P:(h + 1) * P], wffq[:, h * D:(h + 1) * D], x1T[:],
                                     start=True, stop=True)
                last.then_inc(qT_done, 1)

            def mix(t, h, last_tile):
                n = H * t + h + 1
                pe.wait_ge(weighted, n)
                for k in range(TOPK):
                    last = pe.matmul(psK[:, 0:KV], ident[:], G[:, h % SLOTS, k, :],
                                     start=(k == 0), stop=(k == TOPK - 1))
                last.then_inc(combined, 1)
                pe.wait_ge(kv_copied, n)
                own(pe)
                pe.transpose(psK[0:D, 128:256], kn[:], ident[:]).then_inc(kT_done, 1)
                pe.wait_ge(kT_ready, n)
                if h == 0:
                    pe.wait_ge(qT_ready, t + 1)
                    if not last_tile:
                        pe.wait_ge(sims_ready, t + 2)
                for j in range(2):
                    last = pe.matmul(psS[:, j * 512:(j + 1) * 512], qT[:, h, :], kT[:, h, j * 512:(j + 1) * 512],
                                     start=True, stop=True)
                last.then_inc(s2_done, 1)
                pe.wait_ge(p2_ready, n)
                scores_T(p2T_done)
                pe.wait_ge(p2T_ready, n)
                for j in range(TPB):
                    last = pe.matmul(psO[:, h * D:(h + 1) * D], pT[:, j * P:(j + 1) * P], vs[:, j, h, :],
                                     start=(j == 0), stop=(j == TPB - 1))
                last.then_inc(pv2_done, 1)

            def back(t):
                pe.wait_ge(o_ready, H * t + H)
                for c in range(4):
                    last = pe.transpose(psT[:, c * P:(c + 1) * P], on[:, c * P:(c + 1) * P], ident[:])
                last.then_inc(oT_done, 1)
                pe.wait_ge(oT_ready, t + 1)
                for c in range(4):
                    last = pe.matmul(psF[:, D:2 * D], oT[:, c, :], wo[:, c, :], start=(c == 0), stop=(c == 3))
                last.then_inc(wo_done, 1)

            def tile(t, last_tile):
                queries(t)
                if not last_tile:
                    pe.wait_ge(qT_ready, t + 1)
                    front(t + 1)
                for h in range(H):
                    mix(t, h, last_tile)
                back(t)

            front(0)
            with pe.Fori(0, TILES - 1) as t:
                tile(t, False)
            tile(TILES - 1, True)

        @block.scalar
        def _(act):
            act.wait_ge(prep_pe, 1)
            nc.scalar.copy(weff[:].rearrange("p s o -> p o s"), psS[:, 0:512].rearrange("p (o s) -> p o s", s=STRIDE))
            nc.scalar.copy(msim[:], psT[0:D, :])
            act.wait_ge(zeroed, 4)
            nc.scalar.copy(hn[:], ident[:, 0:D]).then_inc(prep_act, 1)

            def mask_for(t, dst, ready):
                at = (TPB - 1) * P - tile_in_batch(t) * P
                nc.scalar.copy(dst[:], mask[:, bass.ds(at, S)]).then_inc(ready, 1)

            def front(t):
                j = tile_in_batch(t)
                mask_for(t, mask1, mask1_ready)
                act.wait_ge(tok_done, t + 1)
                nc.scalar.copy(hT[0:D, :], psA[0:D, 0:P]).then_inc(hT_ready, 1)
                act.wait_ge(proj_done, t + 1)
                nc.scalar.mul(q1T[:], psA[0:D, 128:256], SCALE)
                nc.scalar.copy(k1T[:, bass.ds(j * P, P)], psA[0:D, 256:384])
                nc.scalar.copy(v1[:, bass.ds(j, 1), :].rearrange("p o d -> p (o d)"), psA[:, 384:448])
                nc.scalar.copy(hn[:], psA[:, 448:512]).then_inc(qkv_ready, 1)
                act.wait_ge(s1_masked, t + 1)
                nc.scalar.activation(prob[:], sm[:], ACT.Exp, bias=col[:, 1:2], accum_out=col[:, 2:3]).then_inc(p1_ready, 1)
                act.wait_ge(p1T_done, t + 1)
                nc.scalar.copy(pT[:], psT[:]).then_inc(p1T_ready, 1)
                act.wait_ge(x1T_done, t + 1)
                nc.scalar.copy(x1T[:], psK[0:D, 256:384]).then_inc(x1T_ready, 1)
                act.wait_ge(sims_done, t + 1)
                nc.scalar.copy(sims[:].rearrange("p a h k -> p (a h k)"), psS[:]).then_inc(sims_ready, 1)

            def route(t, r):
                act.wait_ge(fd_ready, 2 * t + r + 1)
                nc.scalar.activation(fe[:], fd[:], ACT.Exp).then_inc(fe_ready, 1)

            def mix(t, h):
                n = H * t + h + 1
                j = tile_in_batch(t)
                act.wait_ge(combined, n)
                nc.scalar.copy(kn[:], psK[:, 0:D])
                nc.scalar.copy(vs[:, bass.ds(j, 1), h, :].rearrange("p o d -> p (o d)"), psK[:, D:KV]).then_inc(kv_copied, 1)
                act.wait_ge(kT_done, n)
                nc.scalar.copy(kT[:, h, bass.ds(j * P, P)], psK[0:D, 128:256]).then_inc(kT_ready, 1)
                act.wait_ge(s2_masked, n)
                nc.scalar.activation(prob[:], sm[:], ACT.Exp, bias=col2[:, 1:2], accum_out=col2[:, 2:3]).then_inc(p2_ready, 1)
                act.wait_ge(p2T_done, n)
                nc.scalar.copy(pT[:], psT[:]).then_inc(p2T_ready, 1)

            def tile(t, last_tile):
                mask_for(t, mask2, mask2_ready)
                act.wait_ge(qT_done, t + 1)
                nc.scalar.mul(qT[:].rearrange("p h q -> p (h q)"), psT[0:D, :], SCALE).then_inc(qT_ready, 1)
                if not last_tile:
                    front(t + 1)
                for h in range(H):
                    mix(t, h)
                    if h % GROUP == GROUP - 1 and not last_tile:
                        route(t + 1, h // GROUP)
                act.wait_ge(oT_done, t + 1)
                nc.scalar.copy(oT[:].rearrange("p c q -> p (c q)"), psT[:, 0:512]).then_inc(oT_ready, 1)

            front(0)
            for r in range(2):
                route(0, r)
            with act.Fori(0, TILES - 1) as t:
                tile(t, False)
            tile(TILES - 1, True)

        @block.vector
        def _(dve):
            def steps(s, per_call, call):
                k = [0]

                def link(ins):
                    k[0] += 1
                    assert k[0] <= per_call
                    ins.then_inc(s, 1)
                    dve.wait_ge(s, per_call * call + k[0])
                    return ins

                def closed():
                    assert k[0] == per_call, k
                return link, closed

            nc.vector.memset(wtok, 0.0).then_inc(wtok_zeroed, 1)
            nc.vector.memset(k1T[:], 0.0).then_inc(zeroed, 1)
            nc.vector.memset(v1[:], 0.0).then_inc(zeroed, 1)
            nc.vector.memset(hT[D:D + 1, :], 1.0).then_inc(zeroed, 1)

            def norm(link, y, c, dst):
                link(nc.vector.bn_stats(c[:, 4:10], y[:]))
                own(dve)
                link(nc.vector.bn_aggr(c[:, 10:12], c[:, 4:10]))
                v, y0, t = c[:, 13:14], c[:, 12:13], c[:, 14:15]
                link(nc.vector.tensor_scalar(v, c[:, 11:12], EPS, None, ALU.add))
                link(nc.vector.tensor_scalar(y0.bitcast(U32), v.bitcast(U32), -0.5, float(0x5F3759DF), ALU.mult, ALU.add))
                for _ in range(NEWTON):
                    link(nc.vector.scalar_tensor_tensor(out=t, in0=v, scalar=y0, in1=y0, op0=ALU.mult, op1=ALU.mult))
                    link(nc.vector.tensor_scalar(t, t, -0.5, 1.5, ALU.mult, ALU.add))
                    link(nc.vector.tensor_scalar(y0, y0, t, None, ALU.mult))
                return nc.vector.tensor_scalar(dst[:], y[:], c[:, 10:11], c[:, 12:13], ALU.subtract, ALU.mult)

            def masked_max(link, m, c):
                own(dve)
                link(nc.vector.tensor_tensor_reduce(out=sm[:], in0=psS[:], in1=m[:], scale=1.0, scalar=LOW,
                                                    op0=ALU.add, op1=ALU.max, accum_out=c[:, 0:1]))
                return nc.vector.tensor_scalar(c[:, 1:2], c[:, 0:1], -1.0, None, ALU.mult)

            def front(t):
                link, closed = steps(front_step, 3 + NORM_STEPS, t)
                dve.wait_ge(s1_done, t + 1)
                dve.wait_ge(mask1_ready, t + 1)
                masked_max(link, mask1, col).then_inc(s1_masked, 1)
                dve.wait_ge(p1_ready, t + 1)
                link(nc.vector.reciprocal(col[:, 3:4], col[:, 2:3]))
                dve.wait_ge(pv1_done, t + 1)
                link(nc.vector.scalar_tensor_tensor(out=y1[:], in0=psF[:, 0:D], scalar=col[:, 3:4], in1=hn[:],
                                                    op0=ALU.mult, op1=ALU.add))
                norm(link, y1, col, x1).then_inc(x1_ready, 1)
                closed()

            def route(t, r):
                link, closed = steps(route_step, 13, 2 * t + r)
                rows = [(a, g) for a in range(2) for g in range(GROUP)]
                if r == 0:
                    dve.wait_ge(sims_ready, t + 1)
                    own(dve)
                for a, g in rows:
                    last = nc.vector.max(rs[:, a, g, 0:8], sims[:, a, GROUP * r + g, :])
                link(last)
                own(dve)
                for a, g in rows:
                    nc.vector.max_index(ri[:, a, g, 0:8], rs[:, a, g, 0:8], sims[:, a, GROUP * r + g, :])
                for a, g in rows:
                    last = nc.vector.match_replace(rest[:, a, g, :], rs[:, a, g, 0:8], sims[:, a, GROUP * r + g, :], LOW)
                link(last)
                own(dve)
                for a, g in rows:
                    last = nc.vector.max(rs[:, a, g, 8:16], rest[:, a, g, :])
                link(last)
                own(dve)
                for a, g in rows:
                    last = nc.vector.max_index(ri[:, a, g, 8:16], rs[:, a, g, 8:16], rest[:, a, g, :])
                link(last)
                link(nc.vector.scalar_tensor_tensor(
                    out=code1[:].rearrange("p g k -> p (g k)"), in0=ri[:, 1].rearrange("p g k -> p (g k)"),
                    scalar=float(NK), in1=hbase[:, GROUP * r:GROUP * r + GROUP].rearrange("p g k -> p (g k)"),
                    op0=ALU.mult, op1=ALU.add))

                def pairs(dst, row, column):
                    at = 0
                    for r0, nr, n_c in BLOCKS:
                        shape = [P, GROUP, nr, n_c]
                        ins = nc.vector.tensor_tensor(
                            dst[:, :, at:at + nr * n_c].rearrange("p g (r c) -> p g r c", c=n_c),
                            row[:, :, r0:r0 + nr, None].broadcast_to(shape),
                            column[:, :, None, 0:n_c].broadcast_to(shape), ALU.add)
                        at += nr * n_c
                    return ins

                pairs(cs, rs[:, 0], rs[:, 1])
                link(pairs(cc, ri[:, 0], code1[:]))
                own(dve)
                for g in range(GROUP):
                    last = nc.vector.max(fs[:, g, 0:8], cs[:, g, :])
                link(last)
                own(dve)
                for g in range(GROUP):
                    nc.vector.max_index(pos[:, g, 0:8], fs[:, g, 0:8], cs[:, g, :])
                for g in range(GROUP):
                    last = nc.vector.match_replace(cs2[:, g, :], fs[:, g, 0:8], cs[:, g, :], LOW)
                link(last)
                own(dve)
                for g in range(GROUP):
                    last = nc.vector.max(fs[:, g, 8:16], cs2[:, g, :])
                link(last)
                nc.vector.tensor_tensor(fd[:], fs[:], fs[:, :, 0:1].broadcast_to([P, GROUP, TOPK]),
                                        ALU.subtract).then_inc(fd_ready, 1)
                for g in range(GROUP):
                    last = nc.vector.max_index(pos[:, g, 8:16], fs[:, g, 8:16], cs2[:, g, :])
                link(last)
                link(nc.vector.tensor_copy(posb[:], pos[:]))
                shape = [P, GROUP, CAND, TOPK]
                nc.vector.tensor_tensor(eq[:], posb[:, :, None, :].broadcast_to(shape),
                                        iota[:, None, :, :].broadcast_to(shape), ALU.is_equal)
                dve.wait_ge(fe_ready, 2 * t + r + 1)
                link(nc.vector.tensor_reduce(fsum[:, 0, :], fe[:], AX_X, ALU.add))
                nc.vector.reciprocal(fsum[:, 1, :], fsum[:, 0, :])
                link(nc.vector.tensor_tensor(pick[:], eq[:], cc[:, :, :, None].broadcast_to(shape), ALU.mult))
                nc.vector.tensor_tensor(wgt[:, GROUP * r:GROUP * (r + 1), :], fe[:],
                                        fsum[:, 1, :, None].broadcast_to([P, GROUP, TOPK]), ALU.mult)
                with nc.allow_low_precision(reason="whole numbers below 2**15"):
                    nc.vector.tensor_reduce(idx[:, GROUP * r:GROUP * (r + 1), :],
                                            pick[:].rearrange("p g c k -> p g k c"), AX_X, ALU.add).then_inc(routed, 1)
                closed()

            def mix(t, h):
                n = H * t + h + 1
                link, closed = steps(mix_step, 2, n - 1)
                dve.wait_ge(gathered[h % SLOTS], 16 * TOPK * (2 * t + h // SLOTS + 1))
                dve.wait_ge(routed, 2 * t + h // GROUP + 1)
                g = G[:, h % SLOTS]
                nc.vector.tensor_tensor(g, g, wgt[:, h, :, None].broadcast_to([P, TOPK, KV]), ALU.mult).then_inc(weighted, 1)
                dve.wait_ge(s2_done, n)
                if h == 0:
                    dve.wait_ge(mask2_ready, t + 1)
                masked_max(link, mask2, col2).then_inc(s2_masked, 1)
                dve.wait_ge(p2_ready, n)
                link(nc.vector.reciprocal(col2[:, 3:4], col2[:, 2:3]))
                dve.wait_ge(pv2_done, n)
                nc.vector.tensor_scalar(on[:, h * D:(h + 1) * D], psO[:, h * D:(h + 1) * D], col2[:, 3:4], None,
                                        ALU.mult).then_inc(o_ready, 1)
                closed()

            def back(t, last_tile):
                link, closed = steps(back_step, 1 + NORM_STEPS, t)
                if last_tile:
                    dve.wait_ge(stored, 16 * t)
                dve.wait_ge(wo_done, t + 1)
                link(nc.vector.tensor_tensor(y2[:], psF[:, D:2 * D], x1c[:], ALU.add))
                norm(link, y2, col2, yo).then_inc(y_ready, 1)
                closed()

            def tile(t, last_tile):
                dve.wait_ge(x1_ready, t + 1)
                nc.vector.tensor_copy(x1c[:], x1[:])
                if not last_tile:
                    front(t + 1)
                for h in range(H):
                    mix(t, h)
                    if h % GROUP == GROUP - 1 and not last_tile:
                        route(t + 1, h // GROUP)
                back(t, last_tile)

            dve.wait_ge(c_loaded, 16 * (2 + len(consts)))
            front(0)
            for r in range(2):
                route(0, r)
            with dve.Fori(0, TILES - 1) as t:
                tile(t, False)
            tile(TILES - 1, True)


def shape_constants():
    import numpy as np
    f = np.arange(FREQS)[:, None]
    rows = []
    for half in range(2):
        angle = 2 * np.pi * f * (np.arange(STRIDE)[None, :] + STRIDE * half) / PATCH
        rows += [np.cos(angle) / np.sqrt(PATCH), -np.sin(angle) / np.sqrt(PATCH)]
    dft = np.concatenate(rows, 0).astype(np.float32)
    ident = np.eye(P, dtype=np.float32)
    strip = np.where(np.arange(2 * S - P)[None, :] <= S - P + np.arange(P)[:, None], 0.0, NEG).astype(np.float32)
    iota = np.broadcast_to(np.arange(CAND)[None, :, None], (P, CAND, TOPK)).reshape(P, -1)
    hbase = np.broadcast_to((NKV * np.arange(H))[None, :, None], (P, H, TOPK)).reshape(P, -1).astype(np.float32)
    return dft, ident, strip, iota, hbase


def kernel(x, L0_tok_W, L0_attn_Wq, L0_attn_bq, L0_attn_Wk, L0_attn_bk, L0_attn_Wv, L0_attn_bv,
           L0_ffn_Wq_pk, L0_ffn_pk_keys, L0_ffn_Wq, L0_ffn_keys_table, L0_ffn_values_table, L0_ffn_Wo):
    import ml_dtypes
    import numpy as np
    import concourse.bacc as bacc
    from concourse.bass_utils import run_bass_kernel_spmd

    dft, ident, strip, iota, hbase = shape_constants()
    a = np.ascontiguousarray
    qkv = np.stack([np.concatenate([np.asarray(w), np.asarray(b)[None, :]], 0) for w, b in
                    ((L0_attn_Wq, L0_attn_bq), (L0_attn_Wk, L0_attn_bk), (L0_attn_Wv, L0_attn_bv))], 1)
    arrays = {
        "x": a(np.asarray(x).reshape(B, C, T, TPB, VT).transpose(0, 3, 1, 2, 4).reshape(TILES, C, T, VT)),
        "w_tok": a(L0_tok_W),
        "w_qkv": a(qkv),
        "w_pk": a(np.asarray(L0_ffn_Wq_pk).reshape(D, 2 * H, DK).transpose(2, 1, 0)),
        "keys": a(np.asarray(L0_ffn_pk_keys).transpose(3, 0, 2, 1).reshape(DK, 2 * H, NK)),
        "w_q": a(L0_ffn_Wq),
        "table": a(np.concatenate([np.asarray(L0_ffn_keys_table), np.asarray(L0_ffn_values_table)], 1)),
        "w_o": a(L0_ffn_Wo),
        "dft": dft, "ident_d": ident, "mask_d": strip, "iota_d": iota.astype(ml_dtypes.bfloat16), "hbase_d": hbase,
    }
    nc = bacc.Bacc("TRN2", target_bir_lowering=False, num_devices=1)
    aps = {n: nc.dram_tensor(n, v.shape, mybir.dt.from_np(v.dtype), kind="ExternalInput").ap()
           for n, v in arrays.items()}
    out = nc.dram_tensor("out", (TILES, P, D), F32, kind="ExternalOutput").ap()
    build(nc, out=out, **aps)
    r = run_bass_kernel_spmd(nc, [arrays], core_ids=[0])
    return r.results[0]["out"].reshape(B, S, D)
```

```python
from contextlib import ExitStack

import concourse.bass as bass
from concourse import mybir

F32, F16, U32 = mybir.dt.float32, mybir.dt.float16, mybir.dt.uint32
ALU = mybir.AluOpType
ACT = mybir.ActivationFunctionType
AX_X = mybir.AxisListType.X

B, C, T, V = 4, 64, 128, 64
PATCH, STRIDE = 16, 8
N = T // STRIDE
S = V * N
P = 128
TPB = S // P
TILES = B * TPB
VT = P // N
D = 64
FREQS = PATCH // 2 + 1
H, NK, TOPK, DK = 8, 64, 16, 32
NKV = NK * NK
KV = 2 * D
SCALE = D ** -0.5
EPS = 1e-5
NEWTON = 3
NORM_STEPS = 4 + 3 * NEWTON
FRONT_STEPS = 3 + NORM_STEPS
ROUTE_STEPS = 17
NEG = -1e30
LOW = -3e38
SLOTS = 4
GROUP = 4

BLOCKS = [(0, 1, 16), (1, 1, 8), (2, 2, 5), (4, 4, 3), (8, 8, 1)]
CAND = sum(nr * nc_ for _, nr, nc_ in BLOCKS)
PLACES = -(-CAND // 8) * 8
MID = NKV // 2


def build(nc, x, w_tok, w_qkv, w_pk, keys, w_q, table, w_o, dft, ident_d, mask_d, iota_d, hbase_d, out):
    with ExitStack() as ctx:
        def sb(name, shape, dt=F32):
            return ctx.enter_context(nc.sbuf_tensor(name, shape, dt))

        def ps(name, shape):
            return ctx.enter_context(nc.psum_tensor(name, shape, F32))

        def sem(name):
            return ctx.enter_context(nc.semaphore(name))

        ident = sb("ident", [P, P])
        mask = sb("mask", [P, S - P + S])
        iota = sb("iota", [P, PLACES, TOPK], F16)
        hbase = sb("hbase", [P, H, TOPK])
        dftm = sb("dftm", [4 * FREQS, STRIDE])
        weff = sb("weff", [P, STRIDE, D])
        wqkv = sb("wqkv", [D + 1, 3, D])
        wpk = sb("wpk", [DK, 2 * H, D])
        keysT = sb("keysT", [DK, 2 * H, NK])
        msim = sb("msim", [D, 2 * H * NK])
        wffq = sb("wffq", [D, H * D])
        wo = sb("wo", [P, 4, D])
        k1T = sb("k1T", [D, S])
        v1 = sb("v1", [P, TPB, D])
        kT = sb("kT", [D, H, S])
        vs = sb("vs", [P, TPB, H, D])
        xin = sb("xin", [P, T * VT])
        hT = sb("hT", [D + 1, P])
        hn = sb("hn", [P, D])
        q1T = sb("q1T", [D, P])
        mask1 = sb("mask1", [P, S])
        mask2 = sb("mask2", [P, S])
        sm = sb("sm", [P, S])
        prob = sb("prob", [P, S])
        pT = sb("pT", [P, S])
        col = sb("col", [P, 16])
        y1 = sb("y1", [P, D])
        x1 = sb("x1", [P, D])
        x1c = sb("x1c", [P, D])
        x1T = sb("x1T", [D, P])
        sims = sb("sims", [P, 2, H, NK])
        rest = sb("rest", [P, 2, GROUP, NK])
        rs = sb("rs", [P, 2, GROUP, TOPK])
        ri = sb("ri", [P, 2, GROUP, TOPK], U32)
        code1 = sb("code1", [P, GROUP, TOPK])
        cs = sb("cs", [P, GROUP, CAND])
        cs2 = sb("cs2", [P, GROUP, CAND])
        cc = sb("cc", [P, GROUP, CAND])
        fs = sb("fs", [P, GROUP, TOPK])
        fd = sb("fd", [P, GROUP, TOPK])
        fe = sb("fe", [P, GROUP, TOPK])
        pos = sb("pos", [P, GROUP, TOPK], U32)
        posh = sb("posh", [P, GROUP, TOPK], F16)
        eq = sb("eq", [P, GROUP, PLACES, TOPK], F16)
        ccm = sb("ccm", [P, GROUP, PLACES, TOPK], F16)
        picked = sb("picked", [P, GROUP, TOPK])
        fsum = sb("fsum", [P, 2, GROUP])
        idx = sb("idx", [P, H, TOPK], U32)
        wgt = sb("wgt", [P, H, TOPK])
        G = sb("G", [P, SLOTS, TOPK, KV])
        wtok = G[0:4 * FREQS].rearrange("p s k (h c) -> p (s k) (h c)", c=C)
        kvn = sb("kvn", [P, KV])
        qT = sb("qT", [D, H, P])
        on = sb("on", [P, H * D])
        oT = sb("oT", [P, 4, P])
        col2 = [sb(f"col2_{i}", [P, 4]) for i in range(2)]
        colb = sb("colb", [P, 16])
        y2 = sb("y2", [P, D])
        yo = sb("yo", [P, D])

        psS = ps("psS", [P, S])
        psT = ps("psT", [P, S])
        psA = ps("psA", [P, 512])
        psK = ps("psK", [P, 512])
        psO = ps("psO", [P, 512])
        psF = ps("psF", [D, P])

        c_loaded = sem("c_loaded")
        zeroed = sem("zeroed")
        wtok_zeroed = sem("wtok_zeroed")
        prep_pe = sem("prep_pe")
        prep_act = sem("prep_act")
        x_loaded = sem("x_loaded")
        tok_done = sem("tok_done")
        hT_ready = sem("hT_ready")
        proj_done = sem("proj_done")
        qkv_ready = sem("qkv_ready")
        mask1_ready = sem("mask1_ready")
        mask2_ready = sem("mask2_ready")
        s1_done = sem("s1_done")
        s1_masked = sem("s1_masked")
        p1_ready = sem("p1_ready")
        p1T_done = sem("p1T_done")
        p1T_ready = sem("p1T_ready")
        pv1_done = sem("pv1_done")
        x1_ready = sem("x1_ready")
        x1T_done = sem("x1T_done")
        x1T_ready = sem("x1T_ready")
        sims_done = sem("sims_done")
        sims_ready = sem("sims_ready")
        fd_ready = sem("fd_ready")
        fe_ready = sem("fe_ready")
        routed = sem("routed")
        gathered = [sem(f"gathered{i}") for i in range(SLOTS)]
        weighted = sem("weighted")
        combined = sem("combined")
        kv_summed = sem("kv_summed")
        v_ready = sem("v_ready")
        kT_done = sem("kT_done")
        kT_ready = sem("kT_ready")
        qT_done = sem("qT_done")
        qT_ready = sem("qT_ready")
        s2_done = sem("s2_done")
        s2_masked = sem("s2_masked")
        p2_ready = sem("p2_ready")
        p2T_done = sem("p2T_done")
        p2T_ready = sem("p2T_ready")
        pv2_done = sem("pv2_done")
        o_ready = sem("o_ready")
        oT_done = sem("oT_done")
        oT_ready = sem("oT_ready")
        wo_done = sem("wo_done")
        y_ready = sem("y_ready")
        stored = sem("stored")
        yo_free = sem("yo_free")
        cc_ready = sem("cc_ready")
        ccm_ready = sem("ccm_ready")
        front_step = sem("front_step")
        route_step = sem("route_step")
        mix_step = sem("mix_step")
        scores_step = sem("scores_step")
        own_waits = sem("own_waits")
        back_step = sem("back_step")

        consts = [
            (ident[:], ident_d), (mask[:], mask_d), (iota[:].rearrange("p c k -> p (c k)"), iota_d),
            (hbase[:].rearrange("p h k -> p (h k)"), hbase_d), (dftm[:], dft),
            (wqkv[:], w_qkv), (wpk[:], w_pk), (keysT[:], keys), (wffq[:], w_q),
            (wo[:], w_o.rearrange("(c p) o -> p c o", p=P)),
        ]
        w_rows = w_tok.rearrange("o (r c) -> r o c", c=C)
        n_rows = 2 * FREQS

        block = ctx.enter_context(nc.Block())

        def tile_in_batch(t):
            return t % TPB

        def own(engine):
            engine.sem_inc(own_waits, 1)

        @block.sync
        def _(sp):
            def load_x(t):
                src = x[bass.ds(t, 1)].rearrange("o c s v -> (o c) s v")
                view = xin[:].rearrange("p (s v) -> p s v", v=VT)
                sp.dma_start(view[0:C], src).then_inc(x_loaded, 16)
                sp.dma_start(view[C:P, 0:T - STRIDE], src[:, STRIDE:T]).then_inc(x_loaded, 16)
                sp.dma_start(view[C:P, T - STRIDE:T],
                             src[:, T - 1:T].broadcast_to([C, STRIDE, VT])).then_inc(x_loaded, 16)

            load_x(0)
            sp.sem_inc(yo_free, 1)
            sp.wait_ge(wtok_zeroed, 1)
            sp.dma_start(wtok[0:n_rows, :, 0:C], w_rows).then_inc(c_loaded, 16)
            sp.dma_start(wtok[n_rows:2 * n_rows, :, C:P], w_rows).then_inc(c_loaded, 16)
            for dst, src in consts:
                sp.dma_start(dst, src).then_inc(c_loaded, 16)
            sp.wait_ge(tok_done, 1)
            load_x(1)

            def store(t):
                sp.wait_ge(y_ready, t + 1)
                own(sp)
                sp.dma_start(out[bass.ds(t, 1)].rearrange("o p d -> (o p) d"), yo[:]).then_inc(stored, 16)
                sp.wait_ge(stored, 16 * t + 16)
                sp.sem_inc(yo_free, 1)

            with sp.Fori(0, TILES - 2) as t:
                sp.wait_ge(tok_done, t + 2)
                own(sp)
                load_x(t + 2)
                store(t)
            store(TILES - 2)
            store(TILES - 1)

        @block.gpsimd
        def _(pool):
            nc.gpsimd.memset(vs[:], 0.0)
            nc.gpsimd.memset(kT[:], 0.0).then_inc(zeroed, 1)

            def gathers(t, first):
                for h in range(H):
                    if h % GROUP == 0:
                        pool.wait_ge(routed, 2 * t + h // GROUP + 1)
                    if not (first and h < SLOTS):
                        pool.wait_ge(combined, H * t + h - SLOTS + 1)
                    own(pool)
                    for k in range(TOPK):
                        pool.indirect_dma_start(
                            G[:, h % SLOTS, k, :], None, table,
                            bass.IndirectOffsetOnAxis(idx[:, h, k:k + 1], 0),
                        ).then_inc(gathered[h % SLOTS], 16)

            gathers(0, True)
            with pool.Fori(1, TILES) as t:
                gathers(t, False)

        @block.tensor
        def _(pe):
            def scores_T(done):
                for j in range(TPB):
                    last = pe.transpose(psT[:, j * P:(j + 1) * P], prob[:, j * P:(j + 1) * P], ident[:])
                last.then_inc(done, 1)

            pe.wait_ge(c_loaded, 16 * (2 + len(consts)))
            for o in range(D):
                pe.matmul(psS[:, o * STRIDE:(o + 1) * STRIDE], wtok[:, o, :], dftm[:], start=True, stop=True)
            for i in range(2 * H):
                last = pe.matmul(psT[0:D, i * NK:(i + 1) * NK], wpk[:, i, :], keysT[:, i, :], start=True, stop=True)
            last.then_inc(prep_pe, 1)
            pe.wait_ge(prep_act, 1)

            def front_tokens(t):
                pe.wait_ge(x_loaded, 48 * t + 48)
                xv = xin[:].rearrange("p (n s v) -> p s v n", s=STRIDE, v=VT)
                for s in range(STRIDE):
                    last = pe.matmul(psA[0:D, 0:P], weff[:, s, :], xv[:, s], start=(s == 0), stop=(s == STRIDE - 1))
                last.then_inc(tok_done, 1)
                pe.wait_ge(hT_ready, t + 1)
                pe.matmul(psA[0:D, 128:256], wqkv[:, 0, :], hT[:], start=True, stop=True)
                pe.matmul(psA[0:D, 256:384], wqkv[:, 1, :], hT[:], start=True, stop=True)
                pe.matmul(psA[:, 384:448], hT[:], wqkv[:, 2, :], start=True, stop=True)
                pe.transpose(psA[:, 448:512], hT[0:D, :], ident[0:D, 0:D]).then_inc(proj_done, 1)

            def front_attention(t):
                pe.wait_ge(qkv_ready, t + 1)
                for j in range(2):
                    last = pe.matmul(psS[:, j * 512:(j + 1) * 512], q1T[:], k1T[:, j * 512:(j + 1) * 512],
                                     start=True, stop=True)
                last.then_inc(s1_done, 1)
                pe.wait_ge(p1_ready, t + 1)
                scores_T(p1T_done)
                pe.wait_ge(p1T_ready, t + 1)
                for j in range(TPB):
                    last = pe.matmul(psA[:, 0:D], pT[:, j * P:(j + 1) * P], v1[:, j, :],
                                     start=(j == 0), stop=(j == TPB - 1))
                last.then_inc(pv1_done, 1)

            def front_scores(t):
                pe.wait_ge(x1_ready, t + 1)
                own(pe)
                pe.transpose(psA[0:D, 128:256], x1[:], ident[:]).then_inc(x1T_done, 1)
                pe.wait_ge(x1T_ready, t + 1)
                for j in range(2):
                    last = pe.matmul(psS[:, j * 512:(j + 1) * 512], x1T[:], msim[:, j * 512:(j + 1) * 512],
                                     start=True, stop=True)
                last.then_inc(sims_done, 1)
                pe.wait_ge(sims_ready, t + 1)

            def queries(t):
                for h in range(H):
                    last = pe.matmul(psT[0:D, h * P:(h + 1) * P], wffq[:, h * D:(h + 1) * D], x1T[:],
                                     start=True, stop=True)
                last.then_inc(qT_done, 1)
                pe.wait_ge(qT_ready, t + 1)

            def slot(new, old, first_tile=False):
                if old:
                    t, h = old
                    pe.wait_ge(kT_ready, H * t + h + 1)
                    for j in range(2):
                        last = pe.matmul(psS[:, j * 512:(j + 1) * 512], qT[:, h, :], kT[:, h, j * 512:(j + 1) * 512],
                                         start=True, stop=True)
                    last.then_inc(s2_done, 1)
                if new:
                    t, h = new
                    pe.wait_ge(weighted, H * t + h + 1)
                    rows = G[:, h % SLOTS].rearrange("p k d -> p (k d)")
                    for k in range(4):
                        last = pe.matmul(psK[:], ident[:], rows[:, k * 512:(k + 1) * 512], start=(k == 0), stop=(k == 3))
                    last.then_inc(combined, 1)
                if old:
                    t, h = old
                    pe.wait_ge(p2_ready, H * t + h + 1)
                    scores_T(p2T_done)
                if new:
                    t, h = new
                    pe.wait_ge(kv_summed, H * t + h + 1)
                    own(pe)
                    pe.transpose(psF[:], kvn[:, 0:D], ident[:]).then_inc(kT_done, 1)
                if old:
                    t, h = old
                    pe.wait_ge(p2T_ready, H * t + h + 1)
                    pe.wait_ge(v_ready, H * t + h + 1)
                    if not (first_tile and h == 0):
                        pe.wait_ge(o_ready, H * t + h)
                    for j in range(TPB):
                        last = pe.matmul(psO[:, h % 2 * D:(h % 2 + 1) * D], pT[:, j * P:(j + 1) * P], vs[:, j, h, :],
                                         start=(j == 0), stop=(j == TPB - 1))
                    last.then_inc(pv2_done, 1)

            def back(t):
                pe.wait_ge(o_ready, H * t + H)
                for c in range(4):
                    last = pe.transpose(psT[:, c * P:(c + 1) * P], on[:, c * P:(c + 1) * P], ident[:])
                last.then_inc(oT_done, 1)
                pe.wait_ge(oT_ready, t + 1)
                for c in range(4):
                    last = pe.matmul(psO[:, 2 * D:3 * D], oT[:, c, :], wo[:, c, :], start=(c == 0), stop=(c == 3))
                last.then_inc(wo_done, 1)

            def tile(t, first_tile=False, last_tile=False):
                for h in range(H):
                    slot((t, h), (t, h - 1) if h else None if first_tile else (t - 1, H - 1), first_tile)
                    if h == 0:
                        queries(t)
                    if h == 1 and not first_tile:
                        back(t - 1)
                    if not last_tile:
                        if h == 1:
                            front_tokens(t + 1)
                        if h == 2:
                            front_attention(t + 1)
                        if h == 3:
                            front_scores(t + 1)

            front_tokens(0)
            front_attention(0)
            front_scores(0)
            tile(0, first_tile=True)
            with pe.Fori(1, TILES - 1) as t:
                tile(t)
            tile(TILES - 1, last_tile=True)
            slot(None, (TILES - 1, H - 1))
            back(TILES - 1)

        @block.scalar
        def _(act):
            act.wait_ge(prep_pe, 1)
            nc.scalar.copy(weff[:].rearrange("p s o -> p o s"), psS[:, 0:512].rearrange("p (o s) -> p o s", s=STRIDE))
            nc.scalar.copy(msim[:], psT[0:D, :])
            act.wait_ge(zeroed, 4)
            nc.scalar.copy(hn[:], ident[:, 0:D]).then_inc(prep_act, 1)

            def mask_for(t, dst, ready):
                at = (TPB - 1) * P - tile_in_batch(t) * P
                nc.scalar.copy(dst[:], mask[:, bass.ds(at, S)]).then_inc(ready, 1)

            def front_tokens(t):
                j = tile_in_batch(t)
                mask_for(t, mask1, mask1_ready)
                act.wait_ge(tok_done, t + 1)
                nc.scalar.copy(hT[0:D, :], psA[0:D, 0:P]).then_inc(hT_ready, 1)
                act.wait_ge(proj_done, t + 1)
                nc.scalar.mul(q1T[:], psA[0:D, 128:256], SCALE)
                nc.scalar.copy(k1T[:, bass.ds(j * P, P)], psA[0:D, 256:384])
                nc.scalar.copy(v1[:, bass.ds(j, 1), :].rearrange("p o d -> p (o d)"), psA[:, 384:448])
                nc.scalar.copy(hn[:], psA[:, 448:512]).then_inc(qkv_ready, 1)

            def front_attention(t):
                act.wait_ge(s1_masked, t + 1)
                nc.scalar.activation(prob[:], sm[:], ACT.Exp, bias=col[:, 1:2], accum_out=col[:, 2:3]).then_inc(p1_ready, 1)
                act.wait_ge(p1T_done, t + 1)
                nc.scalar.copy(pT[:], psT[:]).then_inc(p1T_ready, 1)

            def front_scores(t):
                act.wait_ge(x1T_done, t + 1)
                nc.scalar.copy(x1T[:], psA[0:D, 128:256]).then_inc(x1T_ready, 1)
                act.wait_ge(sims_done, t + 1)
                nc.scalar.copy(sims[:].rearrange("p a h k -> p (a h k)"), psS[:]).then_inc(sims_ready, 1)

            def route(t, r):
                act.wait_ge(cc_ready, 2 * t + r + 1)
                nc.scalar.copy(ccm[:, :, 0:CAND, :], cc[:, :, :, None].broadcast_to([P, GROUP, CAND, TOPK])).then_inc(ccm_ready, 1)
                act.wait_ge(fd_ready, 2 * t + r + 1)
                nc.scalar.activation(fe[:], fd[:], ACT.Exp).then_inc(fe_ready, 1)

            def queries(t):
                mask_for(t, mask2, mask2_ready)
                act.wait_ge(qT_done, t + 1)
                nc.scalar.mul(qT[:].rearrange("p h q -> p (h q)"), psT[0:D, :], SCALE).then_inc(qT_ready, 1)

            def slot(new, old):
                if old:
                    t, h = old
                    c = col2[h % 2]
                    act.wait_ge(s2_masked, H * t + h + 1)
                    nc.scalar.activation(prob[:], sm[:], ACT.Exp, bias=c[:, 1:2], accum_out=c[:, 2:3]).then_inc(p2_ready, 1)
                if new:
                    t, h = new
                    act.wait_ge(kv_summed, H * t + h + 1)
                    nc.scalar.copy(vs[:, bass.ds(tile_in_batch(t), 1), h, :].rearrange("p o d -> p (o d)"),
                                   kvn[:, D:KV]).then_inc(v_ready, 1)
                if old:
                    t, h = old
                    act.wait_ge(p2T_done, H * t + h + 1)
                    nc.scalar.copy(pT[:], psT[:]).then_inc(p2T_ready, 1)
                if new:
                    t, h = new
                    act.wait_ge(kT_done, H * t + h + 1)
                    nc.scalar.copy(kT[:, h, bass.ds(tile_in_batch(t) * P, P)], psF[:]).then_inc(kT_ready, 1)

            def back(t):
                act.wait_ge(oT_done, t + 1)
                nc.scalar.copy(oT[:].rearrange("p c q -> p (c q)"), psT[:, 0:512]).then_inc(oT_ready, 1)

            def tile(t, first_tile=False, last_tile=False):
                for h in range(H):
                    slot((t, h), (t, h - 1) if h else None if first_tile else (t - 1, H - 1))
                    if h == 0:
                        queries(t)
                    if h == 1 and not first_tile:
                        back(t - 1)
                    if not last_tile:
                        if h == 1:
                            front_tokens(t + 1)
                        if h == 2:
                            front_attention(t + 1)
                        if h == 3:
                            front_scores(t + 1)
                        if h == 4 or h == 6:
                            route(t + 1, (h - 4) // 2)

            front_tokens(0)
            front_attention(0)
            front_scores(0)
            route(0, 0)
            route(0, 1)
            tile(0, first_tile=True)
            with act.Fori(1, TILES - 1) as t:
                tile(t)
            tile(TILES - 1, last_tile=True)
            slot(None, (TILES - 1, H - 1))
            back(TILES - 1)

        @block.vector
        def _(dve):
            def steps(s, per_call, call, first=0, last=None):
                k = [first]

                def link(ins):
                    k[0] += 1
                    assert k[0] <= per_call
                    ins.then_inc(s, 1)
                    dve.wait_ge(s, per_call * call + k[0])
                    return ins

                def closed():
                    assert k[0] == (per_call if last is None else last), k
                return link, closed

            nc.vector.memset(wtok, 0.0).then_inc(wtok_zeroed, 1)
            nc.vector.memset(k1T[:], 0.0).then_inc(zeroed, 1)
            nc.vector.memset(v1[:], 0.0).then_inc(zeroed, 1)
            nc.vector.memset(hT[D:D + 1, :], 1.0)
            nc.vector.memset(ccm[:], 0.0).then_inc(zeroed, 1)

            def norm(link, y, c, dst):
                link(nc.vector.bn_stats(c[:, 4:10], y[:]))
                own(dve)
                link(nc.vector.bn_aggr(c[:, 10:12], c[:, 4:10]))
                v, y0, t = c[:, 13:14], c[:, 12:13], c[:, 14:15]
                link(nc.vector.tensor_scalar(v, c[:, 11:12], EPS, None, ALU.add))
                link(nc.vector.tensor_scalar(y0.bitcast(U32), v.bitcast(U32), -0.5, float(0x5F3759DF), ALU.mult, ALU.add))
                for _ in range(NEWTON):
                    link(nc.vector.scalar_tensor_tensor(out=t, in0=v, scalar=y0, in1=y0, op0=ALU.mult, op1=ALU.mult))
                    link(nc.vector.tensor_scalar(t, t, -0.5, 1.5, ALU.mult, ALU.add))
                    link(nc.vector.tensor_scalar(y0, y0, t, None, ALU.mult))
                return nc.vector.tensor_scalar(dst[:], y[:], c[:, 10:11], c[:, 12:13], ALU.subtract, ALU.mult)

            def masked_max(link, m, c):
                own(dve)
                link(nc.vector.tensor_tensor_reduce(out=sm[:], in0=psS[:], in1=m[:], scale=1.0, scalar=LOW,
                                                    op0=ALU.add, op1=ALU.max, accum_out=c[:, 0:1]))
                return nc.vector.tensor_scalar(c[:, 1:2], c[:, 0:1], -1.0, None, ALU.mult)

            def front_attention(t):
                link, closed = steps(front_step, FRONT_STEPS, t, 0, 1)
                dve.wait_ge(s1_done, t + 1)
                dve.wait_ge(mask1_ready, t + 1)
                masked_max(link, mask1, col).then_inc(s1_masked, 1)
                closed()

            def front_scores(t):
                link, closed = steps(front_step, FRONT_STEPS, t, 1)
                dve.wait_ge(p1_ready, t + 1)
                link(nc.vector.reciprocal(col[:, 3:4], col[:, 2:3]))
                dve.wait_ge(pv1_done, t + 1)
                link(nc.vector.scalar_tensor_tensor(out=y1[:], in0=psA[:, 0:D], scalar=col[:, 3:4], in1=hn[:],
                                                    op0=ALU.mult, op1=ALU.add))
                norm(link, y1, col, x1).then_inc(x1_ready, 1)
                closed()

            rows = [(a, g) for a in range(2) for g in range(GROUP)]

            def route_keys(t, r):
                link, closed = steps(route_step, ROUTE_STEPS, 2 * t + r, 0, 6)
                if r == 0:
                    dve.wait_ge(sims_ready, t + 1)
                    own(dve)
                for a, g in rows:
                    last = nc.vector.max(rs[:, a, g, 0:8], sims[:, a, GROUP * r + g, :])
                link(last)
                own(dve)
                for a, g in rows:
                    nc.vector.max_index(ri[:, a, g, 0:8], rs[:, a, g, 0:8], sims[:, a, GROUP * r + g, :])
                for a, g in rows:
                    last = nc.vector.match_replace(rest[:, a, g, :], rs[:, a, g, 0:8], sims[:, a, GROUP * r + g, :], LOW)
                link(last)
                own(dve)
                for a, g in rows:
                    last = nc.vector.max(rs[:, a, g, 8:16], rest[:, a, g, :])
                link(last)
                own(dve)
                for a, g in rows:
                    last = nc.vector.max_index(ri[:, a, g, 8:16], rs[:, a, g, 8:16], rest[:, a, g, :])
                link(last)
                link(nc.vector.tensor_scalar(code1[:], ri[:, 1], float(NK), float(-MID), ALU.mult, ALU.add))

                def pairs(dst, row, column):
                    at = 0
                    for r0, nr, n_c in BLOCKS:
                        shape = [P, GROUP, nr, n_c]
                        ins = nc.vector.tensor_tensor(
                            dst[:, :, at:at + nr * n_c].rearrange("p g (r c) -> p g r c", c=n_c),
                            row[:, :, r0:r0 + nr, None].broadcast_to(shape),
                            column[:, :, None, 0:n_c].broadcast_to(shape), ALU.add)
                        at += nr * n_c
                    return ins

                pairs(cc, ri[:, 0], code1[:]).then_inc(cc_ready, 1)
                link(pairs(cs, rs[:, 0], rs[:, 1]))
                closed()

            def route_pairs(t, r):
                link, closed = steps(route_step, ROUTE_STEPS, 2 * t + r, 6, 11)
                own(dve)
                for g in range(GROUP):
                    last = nc.vector.max(fs[:, g, 0:8], cs[:, g, :])
                link(last)
                own(dve)
                for g in range(GROUP):
                    nc.vector.max_index(pos[:, g, 0:8], fs[:, g, 0:8], cs[:, g, :])
                for g in range(GROUP):
                    last = nc.vector.match_replace(cs2[:, g, :], fs[:, g, 0:8], cs[:, g, :], LOW)
                link(last)
                own(dve)
                for g in range(GROUP):
                    last = nc.vector.max(fs[:, g, 8:16], cs2[:, g, :])
                link(last)
                nc.vector.tensor_tensor(fd[:], fs[:], fs[:, :, 0:1].broadcast_to([P, GROUP, TOPK]),
                                        ALU.subtract).then_inc(fd_ready, 1)
                for g in range(GROUP):
                    last = nc.vector.max_index(pos[:, g, 8:16], fs[:, g, 8:16], cs2[:, g, :])
                link(last)
                link(nc.vector.tensor_copy(posh[:], pos[:]))
                closed()

            def route_rows(t, r):
                link, closed = steps(route_step, ROUTE_STEPS, 2 * t + r, 11)
                heads = slice(GROUP * r, GROUP * (r + 1))
                shape = [P, GROUP, PLACES, TOPK]
                link(nc.vector.tensor_tensor(eq[:], posh[:, :, None, :].broadcast_to(shape),
                                             iota[:, None, :, :].broadcast_to(shape), ALU.is_equal))
                dve.wait_ge(ccm_ready, 2 * t + r + 1)
                link(nc.vector.tensor_tensor(eq[:], eq[:], ccm[:], ALU.mult))
                dve.wait_ge(fe_ready, 2 * t + r + 1)
                nc.vector.tensor_reduce(fsum[:, 0, :], fe[:], AX_X, ALU.add)
                n = PLACES
                for _ in range(3):
                    n //= 2
                    link(nc.vector.tensor_tensor(eq[:, :, 0:n, :], eq[:, :, 0:n, :], eq[:, :, n:2 * n, :], ALU.add))
                nc.vector.reciprocal(fsum[:, 1, :], fsum[:, 0, :])
                link(nc.vector.tensor_reduce(picked[:], eq[:, :, 0:n, :].rearrange("p g c k -> p g k c"), AX_X, ALU.add))
                nc.vector.tensor_tensor(wgt[:, heads, :], fe[:], fsum[:, 1, :, None].broadcast_to([P, GROUP, TOPK]), ALU.mult)
                nc.vector.tensor_tensor(idx[:, heads, :], picked[:], hbase[:, heads, :], ALU.add).then_inc(routed, 1)
                closed()

            def slot(new, old, older):
                if new:
                    t, h = new
                    dve.wait_ge(routed, 2 * t + h // GROUP + 1)
                    dve.wait_ge(gathered[h % SLOTS], 16 * TOPK * (2 * t + h // SLOTS + 1))
                    g = G[:, h % SLOTS]
                    nc.vector.tensor_tensor(g, g, wgt[:, h, :, None].broadcast_to([P, TOPK, KV]), ALU.mult).then_inc(weighted, 1)
                if older:
                    t, h = older
                    c = col2[h % 2]
                    link, closed = steps(mix_step, 1, H * t + h)
                    dve.wait_ge(p2_ready, H * t + h + 1)
                    link(nc.vector.reciprocal(c[:, 3:4], c[:, 2:3]))
                    dve.wait_ge(pv2_done, H * t + h + 1)
                    nc.vector.tensor_scalar(on[:, h * D:(h + 1) * D], psO[:, h % 2 * D:(h % 2 + 1) * D], c[:, 3:4], None,
                                            ALU.mult).then_inc(o_ready, 1)
                    closed()
                if old:
                    t, h = old
                    link, closed = steps(scores_step, 1, H * t + h)
                    dve.wait_ge(s2_done, H * t + h + 1)
                    dve.wait_ge(mask2_ready, t + 1)
                    masked_max(link, mask2, col2[h % 2]).then_inc(s2_masked, 1)
                    closed()
                if new:
                    t, h = new
                    dve.wait_ge(combined, H * t + h + 1)
                    nc.vector.tensor_reduce(kvn[:], psK[:].rearrange("p (k d) -> p d k", d=KV), AX_X, ALU.add)\
                        .then_inc(kv_summed, 1)

            def back(t):
                link, closed = steps(back_step, 1 + NORM_STEPS, t)
                dve.wait_ge(wo_done, t + 1)
                link(nc.vector.tensor_tensor(y2[:], psO[:, 2 * D:3 * D], x1c[:], ALU.add))
                dve.wait_ge(yo_free, t + 1)
                norm(link, y2, colb, yo).then_inc(y_ready, 1)
                closed()

            def tile(t, first_tile=False, last_tile=False):
                for h in range(H):
                    slot((t, h), (t, h - 1) if h else None if first_tile else (t - 1, H - 1),
                         (t, h - 2) if h > 1 else None if first_tile else (t - 1, H - 2 + h))
                    if h == 1 and not first_tile:
                        back(t - 1)
                    if h == 1:
                        dve.wait_ge(x1_ready, t + 1)
                        nc.vector.tensor_copy(x1c[:], x1[:])
                    if not last_tile:
                        if h == 2:
                            front_attention(t + 1)
                        if h == 3:
                            front_scores(t + 1)
                        if h == 4 or h == 6:
                            route_keys(t + 1, (h - 4) // 2)
                            route_pairs(t + 1, (h - 4) // 2)
                        if h == 5 or h == 7:
                            route_rows(t + 1, (h - 5) // 2)

            dve.wait_ge(c_loaded, 16 * (2 + len(consts)))
            front_attention(0)
            front_scores(0)
            for r in range(2):
                route_keys(0, r)
                route_pairs(0, r)
                route_rows(0, r)
            tile(0, first_tile=True)
            with dve.Fori(1, TILES - 1) as t:
                tile(t)
            tile(TILES - 1, last_tile=True)
            slot(None, (TILES - 1, H - 1), (TILES - 1, H - 2))
            slot(None, None, (TILES - 1, H - 1))
            back(TILES - 1)


def shape_constants():
    import numpy as np
    f = np.arange(FREQS)[:, None]
    rows = []
    for half in range(2):
        angle = 2 * np.pi * f * (np.arange(STRIDE)[None, :] + STRIDE * half) / PATCH
        rows += [np.cos(angle) / np.sqrt(PATCH), -np.sin(angle) / np.sqrt(PATCH)]
    dft = np.concatenate(rows, 0).astype(np.float32)
    ident = np.eye(P, dtype=np.float32)
    strip = np.where(np.arange(2 * S - P)[None, :] <= S - P + np.arange(P)[:, None], 0.0, NEG).astype(np.float32)
    iota = np.broadcast_to(np.arange(PLACES)[None, :, None], (P, PLACES, TOPK)).reshape(P, -1).astype(np.float16)
    hbase = np.broadcast_to((MID + NKV * np.arange(H))[None, :, None], (P, H, TOPK)).reshape(P, -1).astype(np.float32)
    return dft, ident, strip, iota, hbase


def kernel(x, L0_tok_W, L0_attn_Wq, L0_attn_bq, L0_attn_Wk, L0_attn_bk, L0_attn_Wv, L0_attn_bv,
           L0_ffn_Wq_pk, L0_ffn_pk_keys, L0_ffn_Wq, L0_ffn_keys_table, L0_ffn_values_table, L0_ffn_Wo):
    import numpy as np
    import concourse.bacc as bacc
    from concourse.bass_utils import run_bass_kernel_spmd

    dft, ident, strip, iota, hbase = shape_constants()
    a = np.ascontiguousarray
    qkv = np.stack([np.concatenate([np.asarray(w), np.asarray(b)[None, :]], 0) for w, b in
                    ((L0_attn_Wq, L0_attn_bq), (L0_attn_Wk, L0_attn_bk), (L0_attn_Wv, L0_attn_bv))], 1)
    arrays = {
        "x": a(np.asarray(x).reshape(B, C, T, TPB, VT).transpose(0, 3, 1, 2, 4).reshape(TILES, C, T, VT)),
        "w_tok": a(L0_tok_W),
        "w_qkv": a(qkv),
        "w_pk": a(np.asarray(L0_ffn_Wq_pk).reshape(D, 2 * H, DK).transpose(2, 1, 0)),
        "keys": a(np.asarray(L0_ffn_pk_keys).transpose(3, 0, 2, 1).reshape(DK, 2 * H, NK)),
        "w_q": a(L0_ffn_Wq),
        "table": a(np.concatenate([np.asarray(L0_ffn_keys_table), np.asarray(L0_ffn_values_table)], 1)),
        "w_o": a(L0_ffn_Wo),
        "dft": dft, "ident_d": ident, "mask_d": strip, "iota_d": iota, "hbase_d": hbase,
    }
    nc = bacc.Bacc("TRN2", target_bir_lowering=False, num_devices=1)
    aps = {n: nc.dram_tensor(n, v.shape, mybir.dt.from_np(v.dtype), kind="ExternalInput").ap()
           for n, v in arrays.items()}
    out = nc.dram_tensor("out", (TILES, P, D), F32, kind="ExternalOutput").ap()
    build(nc, out=out, **aps)
    r = run_bass_kernel_spmd(nc, [arrays], core_ids=[0])
    return r.results[0]["out"].reshape(B, S, D)
```

```python
from contextlib import ExitStack

import concourse.bass as bass
from concourse import mybir

F32, F16, U32 = mybir.dt.float32, mybir.dt.float16, mybir.dt.uint32
ALU = mybir.AluOpType
ACT = mybir.ActivationFunctionType
AX_X = mybir.AxisListType.X

B, C, T, V = 4, 64, 128, 64
PATCH, STRIDE = 16, 8
N = T // STRIDE
S = V * N
P = 128
TPB = S // P
TILES = B * TPB
VT = P // N
D = 64
FREQS = PATCH // 2 + 1
H, NK, TOPK, DK = 8, 64, 16, 32
NKV = NK * NK
KV = 2 * D
SCALE = D ** -0.5
EPS = 1e-5
WARM_UP = 40
NEWTON = 3
NORM_STEPS = 4 + 3 * NEWTON
FRONT_STEPS = 3 + NORM_STEPS
ROUTE_STEPS = 17
BY_DVE = D * 2 // 3
NEG = -1e30
LOW = -3e38
SLOTS = 4
GROUP = 4
LANES = 4

BLOCKS = [(0, 1, 16), (1, 1, 8), (2, 2, 5), (4, 4, 3), (8, 8, 1)]
CAND = sum(nr * nc_ for _, nr, nc_ in BLOCKS)
PLACES = -(-CAND // 8) * 8
MID = NKV // 2


def build(nc, x, w_tok, w_qkv, w_pk, keys, w_q, table, w_o, dft, ident_d, mask_d, iota_d, hbase_d, out):
    with ExitStack() as ctx:
        def sb(name, shape, dt=F32):
            return ctx.enter_context(nc.sbuf_tensor(name, shape, dt))

        def ps(name, shape):
            return ctx.enter_context(nc.psum_tensor(name, shape, F32))

        def sem(name):
            return ctx.enter_context(nc.semaphore(name))

        ident = sb("ident", [P, P])
        warm = sb("warm", [P, 512], F16)
        mask = sb("mask", [P, S - P + S])
        iota = sb("iota", [P, PLACES, TOPK], F16)
        hbase = sb("hbase", [P, H, TOPK])
        dftm = sb("dftm", [4 * FREQS, STRIDE])
        weff = sb("weff", [P, STRIDE, D])
        wqkv = sb("wqkv", [D + 1, 3, D])
        wpk = sb("wpk", [DK, 2 * H, D])
        keysT = sb("keysT", [DK, 2 * H, NK])
        msim = sb("msim", [D, 2 * H * NK])
        wffq = sb("wffq", [D, H * D])
        wo = sb("wo", [P, 4, D])
        k1T = sb("k1T", [D, S])
        v1 = sb("v1", [P, TPB, D])
        kT = sb("kT", [D, H, S])
        vs = sb("vs", [P, TPB, H, D])
        xin = sb("xin", [P, T * VT])
        hT = sb("hT", [D + 1, P])
        hn = sb("hn", [P, D])
        q1T = sb("q1T", [D, P])
        mask1 = sb("mask1", [P, S])
        mask2 = sb("mask2", [P, S])
        sm1 = sb("sm1", [P, S])
        prob1 = sb("prob1", [P, S])
        pT1 = sb("pT1", [P, S])
        col = sb("col", [P, 16])
        y1 = sb("y1", [P, D])
        x1 = sb("x1", [P, D])
        x1c = sb("x1c", [P, D])
        x1T = sb("x1T", [D, P])
        sims = sb("sims", [P, 2, H, NK])
        rest = sb("rest", [P, 2, GROUP, NK])
        rs = sb("rs", [P, 2, GROUP, TOPK])
        ri = sb("ri", [P, 2, GROUP, TOPK], U32)
        code1 = sb("code1", [P, GROUP, TOPK])
        cs = sb("cs", [P, GROUP, CAND])
        cs2 = sb("cs2", [P, GROUP, CAND])
        cc = sb("cc", [P, GROUP, CAND])
        fs = sb("fs", [P, GROUP, TOPK])
        fd = sb("fd", [P, GROUP, TOPK])
        fe = sb("fe", [P, GROUP, TOPK])
        pos = sb("pos", [P, GROUP, TOPK], U32)
        posh = sb("posh", [P, GROUP, TOPK], F16)
        eq = sb("eq", [P, GROUP, PLACES, TOPK], F16)
        ccm = sb("ccm", [P, GROUP, PLACES, TOPK], F16)
        picked = sb("picked", [P, GROUP, TOPK])
        fsum = sb("fsum", [P, 2, GROUP])
        idx = sb("idx", [P, H, TOPK], U32)
        wgt = sb("wgt", [P, H, TOPK])
        G = sb("G", [P, SLOTS, TOPK, KV])
        wtok = G[0:4 * FREQS].rearrange("p s k (h c) -> p (s k) (h c)", c=C)
        part = sb("part", [P, LANES, KV])
        kvn = [sb(f"kvn_{i}", [P, KV]) for i in range(2)]
        qT = sb("qT", [D, H, P])
        sm = sb("sm", [P, S])
        prob = sb("prob", [P, S])
        pT = sb("pT", [P, S])
        on = sb("on", [P, H * D])
        oT = sb("oT", [P, 4, P])
        col2 = [sb(f"col2_{i}", [P, 4]) for i in range(2)]
        colb = sb("colb", [P, 16])
        y2 = sb("y2", [P, D])
        yo = sb("yo", [P, D])

        psS = ps("psS", [P, S])
        psT = ps("psT", [P, S])
        psA = ps("psA", [P, S])
        psO = ps("psO", [P, 512])
        psF = ps("psF", [D, P])

        c_loaded = sem("c_loaded")
        zeroed = sem("zeroed")
        wtok_zeroed = sem("wtok_zeroed")
        warm_ready = sem("warm_ready")
        prep_pe = sem("prep_pe")
        prep_act = sem("prep_act")
        x_loaded = sem("x_loaded")
        tok_done = sem("tok_done")
        hT_ready = sem("hT_ready")
        proj_done = sem("proj_done")
        qkv_ready = sem("qkv_ready")
        mask1_ready = sem("mask1_ready")
        mask2_ready = sem("mask2_ready")
        s1_done = sem("s1_done")
        s1_masked = sem("s1_masked")
        p1_ready = sem("p1_ready")
        p1T_done = sem("p1T_done")
        p1T_ready = sem("p1T_ready")
        pv1_done = sem("pv1_done")
        x1_ready = sem("x1_ready")
        x1T_done = sem("x1T_done")
        x1T_ready = sem("x1T_ready")
        sims_done = sem("sims_done")
        sims_ready = sem("sims_ready")
        fd_ready = sem("fd_ready")
        fe_ready = sem("fe_ready")
        routed = sem("routed")
        gathered = [sem(f"gathered{i}") for i in range(SLOTS)]
        rows_used = sem("rows_used")
        sum_step = sem("sum_step")
        kv_summed = sem("kv_summed")
        v_ready = sem("v_ready")
        kT_done = sem("kT_done")
        kT_ready = sem("kT_ready")
        qT_done = sem("qT_done")
        qT_ready = sem("qT_ready")
        s2_done = sem("s2_done")
        s2_masked = sem("s2_masked")
        p2_ready = sem("p2_ready")
        p2T_done = sem("p2T_done")
        p2T_ready = sem("p2T_ready")
        pv2_done = sem("pv2_done")
        o_ready = sem("o_ready")
        oT_done = sem("oT_done")
        oT_ready = sem("oT_ready")
        wo_done = sem("wo_done")
        y_ready = sem("y_ready")
        stored = sem("stored")
        yo_free = sem("yo_free")
        cc_ready = sem("cc_ready")
        ccm_ready = sem("ccm_ready")
        front_step = sem("front_step")
        route_step = sem("route_step")
        mix_step = sem("mix_step")
        scores_step = sem("scores_step")
        own_waits = sem("own_waits")
        back_step = sem("back_step")

        consts = [
            (ident[:], ident_d), (mask[:], mask_d), (iota[:].rearrange("p c k -> p (c k)"), iota_d),
            (hbase[:].rearrange("p h k -> p (h k)"), hbase_d), (dftm[:], dft),
            (wqkv[:], w_qkv), (wpk[:], w_pk), (keysT[:], keys), (wffq[:], w_q),
            (wo[:], w_o.rearrange("(c p) o -> p c o", p=P)),
        ]
        w_rows = w_tok.rearrange("o (r c) -> r o c", c=C)
        n_rows = 2 * FREQS

        block = ctx.enter_context(nc.Block())

        def tile_in_batch(t):
            return t % TPB

        def own(engine):
            engine.sem_inc(own_waits, 1)

        @block.sync
        def _(sp):
            def load_x(t):
                src = x[bass.ds(t, 1)].rearrange("o c s v -> (o c) s v")
                view = xin[:].rearrange("p (s v) -> p s v", v=VT)
                sp.dma_start(view[0:C], src).then_inc(x_loaded, 16)
                sp.dma_start(view[C:P, 0:T - STRIDE], src[:, STRIDE:T]).then_inc(x_loaded, 16)
                sp.dma_start(view[C:P, T - STRIDE:T],
                             src[:, T - 1:T].broadcast_to([C, STRIDE, VT])).then_inc(x_loaded, 16)

            load_x(0)
            sp.sem_inc(yo_free, 1)
            for dst, src in consts:
                sp.dma_start(dst, src).then_inc(c_loaded, 16)
            sp.wait_ge(wtok_zeroed, 2)
            sp.dma_start(wtok[0:n_rows, :, 0:C], w_rows).then_inc(c_loaded, 16)
            sp.dma_start(wtok[n_rows:2 * n_rows, :, C:P], w_rows).then_inc(c_loaded, 16)
            sp.wait_ge(tok_done, 1)
            load_x(1)

            def store(t):
                sp.wait_ge(y_ready, t + 1)
                own(sp)
                sp.dma_start(out[bass.ds(t, 1)].rearrange("o p d -> (o p) d"), yo[:]).then_inc(stored, 16)
                sp.wait_ge(stored, 16 * t + 16)
                sp.sem_inc(yo_free, 1)

            with sp.Fori(0, TILES - 2) as t:
                sp.wait_ge(tok_done, t + 2)
                own(sp)
                load_x(t + 2)
                store(t)
            store(TILES - 2)
            store(TILES - 1)

        @block.gpsimd
        def _(pool):
            nc.gpsimd.memset(wtok[:, BY_DVE:], 0.0).then_inc(wtok_zeroed, 1)
            nc.gpsimd.memset(vs[:], 0.0)
            nc.gpsimd.memset(kT[:], 0.0).then_inc(zeroed, 1)

            def gathers(t, first):
                for h in range(H):
                    if h % GROUP == 0:
                        pool.wait_ge(routed, 2 * t + h // GROUP + 1)
                    if not (first and h < SLOTS):
                        pool.wait_ge(rows_used, H * t + h - SLOTS + 1)
                    own(pool)
                    for k in range(TOPK):
                        pool.indirect_dma_start(
                            G[:, h % SLOTS, k, :], None, table,
                            bass.IndirectOffsetOnAxis(idx[:, h, k:k + 1], 0),
                        ).then_inc(gathered[h % SLOTS], 16)

            gathers(0, True)
            with pool.Fori(1, TILES) as t:
                gathers(t, False)

        @block.tensor
        def _(pe):
            def scores_T(probs, done):
                for j in range(TPB):
                    last = pe.transpose(psT[:, j * P:(j + 1) * P], probs[:, j * P:(j + 1) * P], ident[:])
                last.then_inc(done, 1)

            pe.wait_ge(warm_ready, 1)
            for _ in range(WARM_UP):
                pe.matmul(psO[:], warm[:, 0:P], warm[:], start=True, stop=True)
            pe.wait_ge(c_loaded, 16 * (2 + len(consts)))
            for o in range(D):
                last = pe.matmul(psS[:, o * STRIDE:(o + 1) * STRIDE], wtok[:, o, :], dftm[:], start=True, stop=True)
            last.then_inc(prep_pe, 1)
            for i in range(2 * H):
                last = pe.matmul(psT[0:D, i * NK:(i + 1) * NK], wpk[:, i, :], keysT[:, i, :], start=True, stop=True)
            last.then_inc(prep_pe, 1)
            pe.wait_ge(prep_act, 1)

            def front_tokens(t):
                pe.wait_ge(x_loaded, 48 * t + 48)
                xv = xin[:].rearrange("p (n s v) -> p s v n", s=STRIDE, v=VT)
                for s in range(STRIDE):
                    last = pe.matmul(psA[0:D, 0:P], weff[:, s, :], xv[:, s], start=(s == 0), stop=(s == STRIDE - 1))
                last.then_inc(tok_done, 1)
                pe.wait_ge(hT_ready, t + 1)
                pe.matmul(psA[0:D, 128:256], wqkv[:, 0, :], hT[:], start=True, stop=True)
                pe.matmul(psA[0:D, 256:384], wqkv[:, 1, :], hT[:], start=True, stop=True)
                pe.matmul(psA[:, 384:448], hT[:], wqkv[:, 2, :], start=True, stop=True)
                pe.transpose(psA[:, 448:512], hT[0:D, :], ident[0:D, 0:D]).then_inc(proj_done, 1)

            def front_attention(t):
                pe.wait_ge(qkv_ready, t + 1)
                for j in range(2):
                    last = pe.matmul(psA[:, j * 512:(j + 1) * 512], q1T[:], k1T[:, j * 512:(j + 1) * 512],
                                     start=True, stop=True)
                last.then_inc(s1_done, 1)
                pe.wait_ge(p1_ready, t + 1)
                scores_T(prob1, p1T_done)
                pe.wait_ge(p1T_ready, t + 1)
                for j in range(TPB):
                    last = pe.matmul(psA[:, 0:D], pT1[:, j * P:(j + 1) * P], v1[:, j, :],
                                     start=(j == 0), stop=(j == TPB - 1))
                last.then_inc(pv1_done, 1)

            def front_scores(t):
                pe.wait_ge(x1_ready, t + 1)
                own(pe)
                pe.transpose(psA[0:D, 128:256], x1[:], ident[:]).then_inc(x1T_done, 1)
                pe.wait_ge(x1T_ready, t + 1)
                for j in range(2):
                    last = pe.matmul(psA[:, j * 512:(j + 1) * 512], x1T[:], msim[:, j * 512:(j + 1) * 512],
                                     start=True, stop=True)
                last.then_inc(sims_done, 1)
                pe.wait_ge(sims_ready, t + 1)

            def queries(t):
                for h in range(H):
                    last = pe.matmul(psT[0:D, h * P:(h + 1) * P], wffq[:, h * D:(h + 1) * D], x1T[:],
                                     start=True, stop=True)
                last.then_inc(qT_done, 1)
                pe.wait_ge(qT_ready, t + 1)

            def slot(new, old, first_tile=False):
                if new:
                    t, h = new
                    pe.wait_ge(kv_summed, H * t + h + 1)
                    own(pe)
                    pe.transpose(psF[:], kvn[h % 2][:, 0:D], ident[:]).then_inc(kT_done, 1)
                if old:
                    t, h = old
                    pe.wait_ge(p2_ready, H * t + h + 1)
                    scores_T(prob, p2T_done)
                if new:
                    t, h = new
                    pe.wait_ge(kT_ready, H * t + h + 1)
                    for j in range(2):
                        last = pe.matmul(psS[:, j * 512:(j + 1) * 512], qT[:, h, :], kT[:, h, j * 512:(j + 1) * 512],
                                         start=True, stop=True)
                    last.then_inc(s2_done, 1)
                if old:
                    t, h = old
                    pe.wait_ge(p2T_ready, H * t + h + 1)
                    pe.wait_ge(v_ready, H * t + h + 1)
                    if not (first_tile and h == 0):
                        pe.wait_ge(o_ready, H * t + h)
                    for j in range(TPB):
                        last = pe.matmul(psO[:, h % 2 * D:(h % 2 + 1) * D], pT[:, j * P:(j + 1) * P], vs[:, j, h, :],
                                         start=(j == 0), stop=(j == TPB - 1))
                    last.then_inc(pv2_done, 1)

            def back(t):
                pe.wait_ge(o_ready, H * t + H)
                for c in range(4):
                    last = pe.transpose(psT[:, c * P:(c + 1) * P], on[:, c * P:(c + 1) * P], ident[:])
                last.then_inc(oT_done, 1)
                pe.wait_ge(oT_ready, t + 1)
                for c in range(4):
                    last = pe.matmul(psO[:, 2 * D:3 * D], oT[:, c, :], wo[:, c, :], start=(c == 0), stop=(c == 3))
                last.then_inc(wo_done, 1)

            def tile(t, first_tile=False, last_tile=False):
                for h in range(H):
                    slot((t, h), (t, h - 1) if h else None if first_tile else (t - 1, H - 1), first_tile)
                    if h == 1 and not first_tile:
                        back(t - 1)
                    if not last_tile:
                        if h == 1:
                            front_tokens(t + 1)
                        if h == 2:
                            front_attention(t + 1)
                        if h == 3:
                            front_scores(t + 1)
                        if h == 7:
                            queries(t + 1)

            front_tokens(0)
            pe.wait_ge(prep_act, 2)
            front_attention(0)
            front_scores(0)
            queries(0)
            tile(0, first_tile=True)
            with pe.Fori(1, TILES - 1) as t:
                tile(t)
            tile(TILES - 1, last_tile=True)
            slot(None, (TILES - 1, H - 1))
            back(TILES - 1)

        @block.scalar
        def _(act):
            act.wait_ge(prep_pe, 1)
            nc.scalar.copy(weff[:].rearrange("p s o -> p o s"), psS[:, 0:512].rearrange("p (o s) -> p o s", s=STRIDE))
            act.wait_ge(zeroed, 4)
            nc.scalar.copy(hn[:], ident[:, 0:D]).then_inc(prep_act, 1)
            act.wait_ge(prep_pe, 2)
            nc.scalar.copy(msim[:], psT[0:D, :]).then_inc(prep_act, 1)

            def mask_for(t, dst, ready):
                at = (TPB - 1) * P - tile_in_batch(t) * P
                nc.scalar.copy(dst[:], mask[:, bass.ds(at, S)]).then_inc(ready, 1)

            def front_tokens(t):
                j = tile_in_batch(t)
                mask_for(t, mask1, mask1_ready)
                act.wait_ge(tok_done, t + 1)
                nc.scalar.copy(hT[0:D, :], psA[0:D, 0:P]).then_inc(hT_ready, 1)
                act.wait_ge(proj_done, t + 1)
                nc.scalar.mul(q1T[:], psA[0:D, 128:256], SCALE)
                nc.scalar.copy(k1T[:, bass.ds(j * P, P)], psA[0:D, 256:384])
                nc.scalar.copy(v1[:, bass.ds(j, 1), :].rearrange("p o d -> p (o d)"), psA[:, 384:448])
                nc.scalar.copy(hn[:], psA[:, 448:512]).then_inc(qkv_ready, 1)

            def front_attention(t):
                act.wait_ge(s1_masked, t + 1)
                nc.scalar.activation(prob1[:], sm1[:], ACT.Exp, bias=col[:, 1:2], accum_out=col[:, 2:3]).then_inc(p1_ready, 1)
                act.wait_ge(p1T_done, t + 1)
                nc.scalar.copy(pT1[:], psT[:]).then_inc(p1T_ready, 1)

            def front_scores(t):
                act.wait_ge(x1T_done, t + 1)
                nc.scalar.copy(x1T[:], psA[0:D, 128:256]).then_inc(x1T_ready, 1)
                act.wait_ge(sims_done, t + 1)
                nc.scalar.copy(sims[:].rearrange("p a h k -> p (a h k)"), psA[:]).then_inc(sims_ready, 1)

            def route_keys(t, r):
                act.wait_ge(cc_ready, 2 * t + r + 1)
                nc.scalar.copy(ccm[:, :, 0:CAND, :], cc[:, :, :, None].broadcast_to([P, GROUP, CAND, TOPK])).then_inc(ccm_ready, 1)

            def route_pairs(t, r):
                act.wait_ge(fd_ready, 2 * t + r + 1)
                nc.scalar.activation(fe[:], fd[:], ACT.Exp).then_inc(fe_ready, 1)

            def queries(t):
                act.wait_ge(qT_done, t + 1)
                nc.scalar.mul(qT[:].rearrange("p h q -> p (h q)"), psT[0:D, :], SCALE).then_inc(qT_ready, 1)

            def slot(new, old):
                if new:
                    t, h = new
                    act.wait_ge(kv_summed, H * t + h + 1)
                    nc.scalar.copy(vs[:, bass.ds(tile_in_batch(t), 1), h, :].rearrange("p o d -> p (o d)"),
                                   kvn[h % 2][:, D:KV]).then_inc(v_ready, 1)
                    act.wait_ge(kT_done, H * t + h + 1)
                    nc.scalar.copy(kT[:, h, bass.ds(tile_in_batch(t) * P, P)], psF[:]).then_inc(kT_ready, 1)
                if old:
                    t, h = old
                    c = col2[h % 2]
                    act.wait_ge(s2_masked, H * t + h + 1)
                    nc.scalar.activation(prob[:], sm[:], ACT.Exp, bias=c[:, 1:2], accum_out=c[:, 2:3]).then_inc(p2_ready, 1)
                    act.wait_ge(p2T_done, H * t + h + 1)
                    nc.scalar.copy(pT[:], psT[:]).then_inc(p2T_ready, 1)

            def back(t):
                act.wait_ge(oT_done, t + 1)
                nc.scalar.copy(oT[:].rearrange("p c q -> p (c q)"), psT[:, 0:512]).then_inc(oT_ready, 1)

            def tile(t, first_tile=False, last_tile=False):
                for h in range(H):
                    slot((t, h), (t, h - 1) if h else None if first_tile else (t - 1, H - 1))
                    if h == 0:
                        mask_for(t, mask2, mask2_ready)
                        route_pairs(t, 1)
                    if h == 1 and not first_tile:
                        back(t - 1)
                    if not last_tile:
                        if h == 1:
                            front_tokens(t + 1)
                        if h == 2:
                            front_attention(t + 1)
                        if h == 3:
                            front_scores(t + 1)
                        if h == 4 or h == 7:
                            route_keys(t + 1, 0 if h == 4 else 1)
                        if h == 4:
                            route_pairs(t + 1, 0)
                        if h == 7:
                            queries(t + 1)

            front_tokens(0)
            front_attention(0)
            front_scores(0)
            queries(0)
            route_keys(0, 0)
            route_pairs(0, 0)
            route_keys(0, 1)
            tile(0, first_tile=True)
            with act.Fori(1, TILES - 1) as t:
                tile(t)
            tile(TILES - 1, last_tile=True)
            slot(None, (TILES - 1, H - 1))
            back(TILES - 1)

        @block.vector
        def _(dve):
            def steps(s, per_call, call, first=0, last=None):
                k = [first]

                def link(ins):
                    k[0] += 1
                    assert k[0] <= per_call
                    ins.then_inc(s, 1)
                    dve.wait_ge(s, per_call * call + k[0])
                    return ins

                def closed():
                    assert k[0] == (per_call if last is None else last), k
                return link, closed

            nc.vector.memset(warm[:], 0.0).then_inc(warm_ready, 1)
            nc.vector.memset(wtok[:, 0:BY_DVE], 0.0).then_inc(wtok_zeroed, 1)
            nc.vector.memset(k1T[:], 0.0).then_inc(zeroed, 1)
            nc.vector.memset(v1[:], 0.0).then_inc(zeroed, 1)
            nc.vector.memset(hT[D:D + 1, :], 1.0)
            nc.vector.memset(ccm[:], 0.0).then_inc(zeroed, 1)

            def norm(link, y, c, dst):
                link(nc.vector.bn_stats(c[:, 4:10], y[:]))
                own(dve)
                link(nc.vector.bn_aggr(c[:, 10:12], c[:, 4:10]))
                v, y0, t = c[:, 13:14], c[:, 12:13], c[:, 14:15]
                link(nc.vector.tensor_scalar(v, c[:, 11:12], EPS, None, ALU.add))
                link(nc.vector.tensor_scalar(y0.bitcast(U32), v.bitcast(U32), -0.5, float(0x5F3759DF), ALU.mult, ALU.add))
                for _ in range(NEWTON):
                    link(nc.vector.scalar_tensor_tensor(out=t, in0=v, scalar=y0, in1=y0, op0=ALU.mult, op1=ALU.mult))
                    link(nc.vector.tensor_scalar(t, t, -0.5, 1.5, ALU.mult, ALU.add))
                    link(nc.vector.tensor_scalar(y0, y0, t, None, ALU.mult))
                return nc.vector.tensor_scalar(dst[:], y[:], c[:, 10:11], c[:, 12:13], ALU.subtract, ALU.mult)

            def masked_max(link, scores, m, dst, c):
                own(dve)
                link(nc.vector.tensor_tensor_reduce(out=dst[:], in0=scores[:], in1=m[:], scale=1.0, scalar=LOW,
                                                    op0=ALU.add, op1=ALU.max, accum_out=c[:, 0:1]))
                return nc.vector.tensor_scalar(c[:, 1:2], c[:, 0:1], -1.0, None, ALU.mult)

            def front_attention(t):
                link, closed = steps(front_step, FRONT_STEPS, t, 0, 1)
                dve.wait_ge(s1_done, t + 1)
                dve.wait_ge(mask1_ready, t + 1)
                masked_max(link, psA, mask1, sm1, col).then_inc(s1_masked, 1)
                closed()

            def front_scores(t):
                link, closed = steps(front_step, FRONT_STEPS, t, 1)
                dve.wait_ge(p1_ready, t + 1)
                link(nc.vector.reciprocal(col[:, 3:4], col[:, 2:3]))
                dve.wait_ge(pv1_done, t + 1)
                link(nc.vector.scalar_tensor_tensor(out=y1[:], in0=psA[:, 0:D], scalar=col[:, 3:4], in1=hn[:],
                                                    op0=ALU.mult, op1=ALU.add))
                norm(link, y1, col, x1).then_inc(x1_ready, 1)
                closed()

            rows = [(a, g) for a in range(2) for g in range(GROUP)]

            def route_keys(t, r):
                link, closed = steps(route_step, ROUTE_STEPS, 2 * t + r, 0, 6)
                if r == 0:
                    dve.wait_ge(sims_ready, t + 1)
                    own(dve)
                for a, g in rows:
                    last = nc.vector.max(rs[:, a, g, 0:8], sims[:, a, GROUP * r + g, :])
                link(last)
                own(dve)
                for a, g in rows:
                    nc.vector.max_index(ri[:, a, g, 0:8], rs[:, a, g, 0:8], sims[:, a, GROUP * r + g, :])
                for a, g in rows:
                    last = nc.vector.match_replace(rest[:, a, g, :], rs[:, a, g, 0:8], sims[:, a, GROUP * r + g, :], LOW)
                link(last)
                own(dve)
                for a, g in rows:
                    last = nc.vector.max(rs[:, a, g, 8:16], rest[:, a, g, :])
                link(last)
                own(dve)
                for a, g in rows:
                    last = nc.vector.max_index(ri[:, a, g, 8:16], rs[:, a, g, 8:16], rest[:, a, g, :])
                link(last)
                link(nc.vector.tensor_scalar(code1[:], ri[:, 1], float(NK), float(-MID), ALU.mult, ALU.add))

                def pairs(dst, row, column):
                    at = 0
                    for r0, nr, n_c in BLOCKS:
                        shape = [P, GROUP, nr, n_c]
                        ins = nc.vector.tensor_tensor(
                            dst[:, :, at:at + nr * n_c].rearrange("p g (r c) -> p g r c", c=n_c),
                            row[:, :, r0:r0 + nr, None].broadcast_to(shape),
                            column[:, :, None, 0:n_c].broadcast_to(shape), ALU.add)
                        at += nr * n_c
                    return ins

                pairs(cc, ri[:, 0], code1[:]).then_inc(cc_ready, 1)
                link(pairs(cs, rs[:, 0], rs[:, 1]))
                closed()

            def route_pairs(t, r):
                link, closed = steps(route_step, ROUTE_STEPS, 2 * t + r, 6, 11)
                own(dve)
                for g in range(GROUP):
                    last = nc.vector.max(fs[:, g, 0:8], cs[:, g, :])
                link(last)
                own(dve)
                for g in range(GROUP):
                    nc.vector.max_index(pos[:, g, 0:8], fs[:, g, 0:8], cs[:, g, :])
                for g in range(GROUP):
                    last = nc.vector.match_replace(cs2[:, g, :], fs[:, g, 0:8], cs[:, g, :], LOW)
                link(last)
                own(dve)
                for g in range(GROUP):
                    last = nc.vector.max(fs[:, g, 8:16], cs2[:, g, :])
                link(last)
                nc.vector.tensor_tensor(fd[:], fs[:], fs[:, :, 0:1].broadcast_to([P, GROUP, TOPK]),
                                        ALU.subtract).then_inc(fd_ready, 1)
                for g in range(GROUP):
                    last = nc.vector.max_index(pos[:, g, 8:16], fs[:, g, 8:16], cs2[:, g, :])
                link(last)
                link(nc.vector.tensor_copy(posh[:], pos[:]))
                closed()

            def route_rows(t, r):
                link, closed = steps(route_step, ROUTE_STEPS, 2 * t + r, 11)
                heads = slice(GROUP * r, GROUP * (r + 1))
                shape = [P, GROUP, PLACES, TOPK]
                link(nc.vector.tensor_tensor(eq[:], posh[:, :, None, :].broadcast_to(shape),
                                             iota[:, None, :, :].broadcast_to(shape), ALU.is_equal))
                dve.wait_ge(ccm_ready, 2 * t + r + 1)
                link(nc.vector.tensor_tensor(eq[:], eq[:], ccm[:], ALU.mult))
                dve.wait_ge(fe_ready, 2 * t + r + 1)
                nc.vector.tensor_reduce(fsum[:, 0, :], fe[:], AX_X, ALU.add)
                n = PLACES
                for _ in range(3):
                    n //= 2
                    link(nc.vector.tensor_tensor(eq[:, :, 0:n, :], eq[:, :, 0:n, :], eq[:, :, n:2 * n, :], ALU.add))
                nc.vector.reciprocal(fsum[:, 1, :], fsum[:, 0, :])
                link(nc.vector.tensor_reduce(picked[:], eq[:, :, 0:n, :].rearrange("p g c k -> p g k c"), AX_X, ALU.add))
                nc.vector.tensor_tensor(wgt[:, heads, :], fe[:], fsum[:, 1, :, None].broadcast_to([P, GROUP, TOPK]), ALU.mult)
                nc.vector.tensor_tensor(idx[:, heads, :], picked[:], hbase[:, heads, :], ALU.add).then_inc(routed, 1)
                closed()

            def slot(new, old, older, meanwhile=None, first_tile=False):
                if new:
                    t, h = new
                    dve.wait_ge(routed, 2 * t + h // GROUP + 1)
                    dve.wait_ge(gathered[h % SLOTS], 16 * TOPK * (2 * t + h // SLOTS + 1))
                    link, closed = steps(sum_step, TOPK // LANES + 1, H * t + h)
                    for k in range(TOPK):
                        row, w, to = G[:, h % SLOTS, k, :], wgt[:, h, k:k + 1], part[:, k % LANES, :]
                        if k < LANES:
                            last = nc.vector.tensor_scalar(to, row, w, None, ALU.mult)
                        else:
                            last = nc.vector.scalar_tensor_tensor(out=to, in0=row, scalar=w, in1=to,
                                                                  op0=ALU.mult, op1=ALU.add)
                        if k % LANES == LANES - 1:
                            link(last)
                    dve.sem_inc(rows_used, 1)
                    link(nc.vector.tensor_tensor(part[:, 0:2, :], part[:, 0:2, :], part[:, 2:4, :], ALU.add))
                    if not (first_tile and h < 2):
                        dve.wait_ge(v_ready, H * t + h - 1)
                        dve.wait_ge(kT_done, H * t + h - 1)
                    nc.vector.tensor_tensor(kvn[h % 2][:], part[:, 0, :], part[:, 1, :], ALU.add).then_inc(kv_summed, 1)
                    closed()
                if old:
                    t, h = old
                    if not (first_tile and h == 0):
                        dve.wait_ge(p2_ready, H * t + h)
                    link, closed = steps(scores_step, 1, H * t + h)
                    dve.wait_ge(s2_done, H * t + h + 1)
                    dve.wait_ge(mask2_ready, t + 1)
                    masked_max(link, psS, mask2, sm, col2[h % 2]).then_inc(s2_masked, 1)
                    closed()
                if older:
                    t, h = older
                    c = col2[h % 2]
                    link, closed = steps(mix_step, 1, H * t + h)
                    dve.wait_ge(p2_ready, H * t + h + 1)
                    link(nc.vector.reciprocal(c[:, 3:4], c[:, 2:3]))
                    dve.wait_ge(pv2_done, H * t + h + 1)
                    nc.vector.tensor_scalar(on[:, h * D:(h + 1) * D], psO[:, h % 2 * D:(h % 2 + 1) * D], c[:, 3:4], None,
                                            ALU.mult).then_inc(o_ready, 1)
                    closed()
                if meanwhile:
                    meanwhile()

            def back(t):
                link, closed = steps(back_step, 1 + NORM_STEPS, t)
                dve.wait_ge(wo_done, t + 1)
                link(nc.vector.tensor_tensor(y2[:], psO[:, 2 * D:3 * D], x1c[:], ALU.add))
                dve.wait_ge(yo_free, t + 1)
                norm(link, y2, colb, yo).then_inc(y_ready, 1)
                closed()

            def tile(t, first_tile=False, last_tile=False):
                for h in range(H):
                    meanwhile = {0: lambda: route_pairs(t, 1), 1: lambda: route_rows(t, 1)}
                    if not last_tile:
                        meanwhile[5] = lambda: route_rows(t + 1, 0)
                        meanwhile[7] = lambda: route_keys(t + 1, 1)
                    slot((t, h), (t, h - 1) if h else None if first_tile else (t - 1, H - 1),
                         (t, h - 2) if h > 1 else None if first_tile else (t - 1, H - 2 + h), meanwhile.get(h), first_tile)
                    if h == 1 and not first_tile:
                        back(t - 1)
                    if h == 1:
                        dve.wait_ge(x1_ready, t + 1)
                        nc.vector.tensor_copy(x1c[:], x1[:])
                    if not last_tile:
                        if h == 2:
                            front_attention(t + 1)
                        if h == 3:
                            front_scores(t + 1)
                        if h == 4:
                            route_keys(t + 1, 0)
                            route_pairs(t + 1, 0)

            dve.wait_ge(c_loaded, 16 * (2 + len(consts)))
            front_attention(0)
            front_scores(0)
            route_keys(0, 0)
            route_pairs(0, 0)
            route_rows(0, 0)
            route_keys(0, 1)
            tile(0, first_tile=True)
            with dve.Fori(1, TILES - 1) as t:
                tile(t)
            tile(TILES - 1, last_tile=True)
            slot(None, (TILES - 1, H - 1), (TILES - 1, H - 2))
            slot(None, None, (TILES - 1, H - 1))
            back(TILES - 1)


def shape_constants():
    import numpy as np
    f = np.arange(FREQS)[:, None]
    rows = []
    for half in range(2):
        angle = 2 * np.pi * f * (np.arange(STRIDE)[None, :] + STRIDE * half) / PATCH
        rows += [np.cos(angle) / np.sqrt(PATCH), -np.sin(angle) / np.sqrt(PATCH)]
    dft = np.concatenate(rows, 0).astype(np.float32)
    ident = np.eye(P, dtype=np.float32)
    strip = np.where(np.arange(2 * S - P)[None, :] <= S - P + np.arange(P)[:, None], 0.0, NEG).astype(np.float32)
    iota = np.broadcast_to(np.arange(PLACES)[None, :, None], (P, PLACES, TOPK)).reshape(P, -1).astype(np.float16)
    hbase = np.broadcast_to((MID + NKV * np.arange(H))[None, :, None], (P, H, TOPK)).reshape(P, -1).astype(np.float32)
    return dft, ident, strip, iota, hbase


def kernel(x, L0_tok_W, L0_attn_Wq, L0_attn_bq, L0_attn_Wk, L0_attn_bk, L0_attn_Wv, L0_attn_bv,
           L0_ffn_Wq_pk, L0_ffn_pk_keys, L0_ffn_Wq, L0_ffn_keys_table, L0_ffn_values_table, L0_ffn_Wo):
    import numpy as np
    import concourse.bacc as bacc
    from concourse.bass_utils import run_bass_kernel_spmd

    dft, ident, strip, iota, hbase = shape_constants()
    a = np.ascontiguousarray
    qkv = np.stack([np.concatenate([np.asarray(w), np.asarray(b)[None, :]], 0) for w, b in
                    ((L0_attn_Wq, L0_attn_bq), (L0_attn_Wk, L0_attn_bk), (L0_attn_Wv, L0_attn_bv))], 1)
    arrays = {
        "x": a(np.asarray(x).reshape(B, C, T, TPB, VT).transpose(0, 3, 1, 2, 4).reshape(TILES, C, T, VT)),
        "w_tok": a(L0_tok_W),
        "w_qkv": a(qkv),
        "w_pk": a(np.asarray(L0_ffn_Wq_pk).reshape(D, 2 * H, DK).transpose(2, 1, 0)),
        "keys": a(np.asarray(L0_ffn_pk_keys).transpose(3, 0, 2, 1).reshape(DK, 2 * H, NK)),
        "w_q": a(L0_ffn_Wq),
        "table": a(np.concatenate([np.asarray(L0_ffn_keys_table), np.asarray(L0_ffn_values_table)], 1)),
        "w_o": a(L0_ffn_Wo),
        "dft": dft, "ident_d": ident, "mask_d": strip, "iota_d": iota, "hbase_d": hbase,
    }
    nc = bacc.Bacc("TRN2", target_bir_lowering=False, num_devices=1)
    aps = {n: nc.dram_tensor(n, v.shape, mybir.dt.from_np(v.dtype), kind="ExternalInput").ap()
           for n, v in arrays.items()}
    out = nc.dram_tensor("out", (TILES, P, D), F32, kind="ExternalOutput").ap()
    build(nc, out=out, **aps)
    r = run_bass_kernel_spmd(nc, [arrays], core_ids=[0])
    return r.results[0]["out"].reshape(B, S, D)
```
